# Optimizing a Trainium2 kernel written in Bass

```python
import numpy as np
import jax
import jax.numpy as jnp

def _softmax(x, axis=-1):
    return jax.nn.softmax(x, axis=axis)

def _gelu(x):
    return jax.nn.gelu(x, approximate=True)

def _silu(x):
    return jax.nn.silu(x)

def _sigmoid(x):
    return jax.nn.sigmoid(x)

def _layernorm(x, axis=-1, eps=1e-05):
    m = jnp.mean(x, axis=axis, keepdims=True)
    v = jnp.var(x, axis=axis, keepdims=True)
    return (x - m) / jnp.sqrt(v + eps)

def _scatter_add(tgt, idx, src, axis=0):
    return tgt.at[idx].add(src)

def _segment_sum(src, seg, n):
    return jax.ops.segment_sum(src, seg, n)
kernel_name = 'mk_macaron_d1_jaxref_r8_a9ba8a'

def setup_inputs(seed: int=0):
    np.random.seed(seed)
    _w = jnp.asarray

    def _L0_attn_setup():
        import jax, jax.numpy as jnp
        import numpy as np
        NUM_HEADS = 16
        key = jax.random.key(seed)
        x = jax.random.normal(key, (4, 256, 128), dtype=jnp.float32)
        return {'x': x}
    _L0_attn_in = _L0_attn_setup()

    def _L0_ffn_setup():
        import jax, jax.numpy as jnp
        import numpy as np
        D_MODEL = 128
        NUM_EXPERTS = 8
        TOP_K = 2
        B, S = (4, 256)
        key = jax.random.key(seed)
        ks = jax.random.split(key, 7)
        scale_in = 1.0 / np.sqrt(D_MODEL)
        scale_hid = 1.0 / np.sqrt(2 * D_MODEL)
        return {'x': jax.random.normal(ks[0], (B, S, D_MODEL), dtype=jnp.float32), 'Wg': jax.random.normal(ks[1], (D_MODEL, NUM_EXPERTS), dtype=jnp.float32) * scale_in, 'bg': jnp.zeros((NUM_EXPERTS,), dtype=jnp.float32), 'W1': jax.random.normal(ks[2], (NUM_EXPERTS, D_MODEL, 2 * D_MODEL), dtype=jnp.float32) * scale_in, 'b1': jnp.zeros((NUM_EXPERTS, 2 * D_MODEL), dtype=jnp.float32), 'W2': jax.random.normal(ks[3], (NUM_EXPERTS, 2 * D_MODEL, D_MODEL), dtype=jnp.float32) * scale_hid, 'b2': jnp.zeros((NUM_EXPERTS, D_MODEL), dtype=jnp.float32)}
    _L0_ffn_in = _L0_ffn_setup()
    _d = {'L0_attn_x': _L0_attn_in['x'], 'L0_ffn_Wg': _L0_ffn_in['Wg'], 'L0_ffn_bg': _L0_ffn_in['bg'], 'L0_ffn_W1': _L0_ffn_in['W1'], 'L0_ffn_b1': _L0_ffn_in['b1'], 'L0_ffn_W2': _L0_ffn_in['W2'], 'L0_ffn_b2': _L0_ffn_in['b2']}
    _x0 = _d['L0_attn_x']
    _d['L0_attn_x'] = jax.random.normal(jax.random.fold_in(jax.random.key(seed), 1), (16, 512, 128), dtype=_x0.dtype)
    del _x0
    return _d

def reference(L0_attn_x, L0_ffn_Wg, L0_ffn_bg, L0_ffn_W1, L0_ffn_b1, L0_ffn_W2, L0_ffn_b2):

    def _L0_attn_ref(x):
        import jax, jax.numpy as jnp
        import numpy as np
        NUM_HEADS = 16
        B, T, D = x.shape
        H = NUM_HEADS
        hd = D // H
        xh = x.reshape(B, T, H, hd)
        x_centered = xh - jnp.mean(xh, axis=1, keepdims=True)
        corr = jnp.einsum('bthd,bThd->bhtT', x_centered, x_centered)
        corr = jax.nn.softmax(corr, axis=-1)
        out = jnp.einsum('bhtT,bThd->bthd', corr, xh)
        return out.reshape(B, T, D)

    def _L0_ffn_ref(x, Wg, bg, W1, b1, W2, b2):
        import jax, jax.numpy as jnp
        import numpy as np
        D_MODEL = 128
        NUM_EXPERTS = 8
        TOP_K = 2
        B, S = (4, 256)
        Bb, Ss, D = x.shape
        E = Wg.shape[1]
        xf = x.reshape(-1, D)
        logits = xf @ Wg + bg
        probs = jax.nn.softmax(logits, axis=-1)
        w, idx = jax.lax.top_k(probs, TOP_K)
        w = w / jnp.sum(w, axis=-1, keepdims=True)
        comb = jnp.sum(jax.nn.one_hot(idx, E, dtype=xf.dtype) * w[..., None], axis=1)
        h = jax.nn.relu(jnp.einsum('nd,edh->enh', xf, W1) + b1[:, None, :])
        y = jnp.einsum('enh,ehd->end', h, W2) + b2[:, None, :]
        out = jnp.einsum('end,ne->nd', y, comb)
        return out.reshape(Bb, Ss, D)
    x = L0_attn_x
    x = x + 0.5 * _L0_ffn_ref(_layernorm(x, axis=-1), L0_ffn_Wg, L0_ffn_bg, L0_ffn_W1, L0_ffn_b1, L0_ffn_W2, L0_ffn_b2)
    x = x + _L0_attn_ref(_layernorm(x, axis=-1))
    x = x + 0.5 * _L0_ffn_ref(_layernorm(x, axis=-1), L0_ffn_Wg, L0_ffn_bg, L0_ffn_W1, L0_ffn_b1, L0_ffn_W2, L0_ffn_b2)
    return x

_drawn_inputs = setup_inputs


def setup_inputs(seed=0):
    import zlib

    import numpy as np

    out = dict(_drawn_inputs(seed))
    spreads = {'L0_ffn_bg': (0.0, 0.1), 'L0_ffn_b1': (0.0, 0.1), 'L0_ffn_b2': (0.0, 0.1)}
    factors = {}
    for name, (base, spread) in spreads.items():
        noise = np.random.default_rng([zlib.crc32(name.encode()), seed]).standard_normal(out[name].shape)
        drawn = base * np.exp(spread * noise) if base else spread * noise
        out[name] = jnp.asarray(drawn.astype(out[name].dtype))
    for name, factor in factors.items():
        out[name] = (out[name] * factor).astype(out[name].dtype)
    return out
```

```python
from contextlib import ExitStack

import concourse.bass as bass
import numpy as np
from concourse import mybir

P = 128
S, T, D = 16, 512, 128
J = T // P
E, F = 8, 256
C = F // P
TOPK = 2
H, HD = 16, 8
Q = 4
G = H // Q
W = P // Q
REP = W // HD
EPS = 1e-5
CENTRED = float(T)
SCORE = 1.0 / CENTRED ** 2
UNIT_ROWS = 4096.0
SHIFT = 50.0

F32, F16, BF16 = mybir.dt.float32, mybir.dt.float16, mybir.dt.bfloat16
ALU = mybir.AluOpType
ACT = mybir.ActivationFunctionType
AX = mybir.AxisListType

IDENT, BLOCK, TRI = 0, P, 2 * P
KEY_LO, QUERY_LO, SHIFT_ROW, KEEP_EVEN, UNIT_EVEN, KEEP_ODD, UNIT_ODD, MINUS_HALF, MINUS_SHIFT = range(
    TRI + E * E, TRI + E * E + 9)
NCONST = TRI + E * E + 9


def constants():
    c = np.zeros((P, NCONST), np.float32)
    row = np.arange(P)
    quadrant, copy = row // W, row % W // HD
    c[:, IDENT:IDENT + P] = np.eye(P)
    c[:, BLOCK:BLOCK + P] = (quadrant[:, None] == quadrant[None, :]) & (copy == 0)[:, None]
    c[:, TRI:TRI + E * E] = (np.arange(E)[None, :] < np.arange(E)[:, None]).reshape(-1)
    c[:, KEY_LO] = -1.0 * (copy == 1)
    c[:, QUERY_LO] = -1.0 * (copy >= 2)
    c[:, SHIFT_ROW] = -1.0 / (UNIT_ROWS * HD) * (copy == 3)
    for odd, keep, unit in ((0, KEEP_EVEN, UNIT_EVEN), (1, KEEP_ODD, UNIT_ODD)):
        c[:, keep] = (quadrant % 2 == odd) & (copy < 3)
        c[:, unit] = UNIT_ROWS * ((quadrant % 2 == odd) & (copy == 3))
    c[:, MINUS_HALF] = -0.5
    c[:, MINUS_SHIFT] = -SHIFT
    return c


def reached(eng, sem, value):
    if not isinstance(value, int) or value > 0:
        eng.wait_ge(sem, value)


def pairs_of_sequences(eng, body):
    n = S // 2
    body(0)
    with eng.Fori(1, n - 1) as i:
        body(i)
    body(n - 1)


def build(nc, x_in, wg_in, bg_in, w1_in, b1_in, w2_in, b2_in, const_in, out):
    with ExitStack() as ctx:
        def sb(name, shape, dt=F32):
            return ctx.enter_context(nc.sbuf_tensor(name, shape, dt))

        def sem(name):
            return ctx.enter_context(nc.semaphore(name))

        X = sb("X", [P, S * J * D])
        W1 = sb("W1", [P, E, F])
        W2 = sb("W2", [P, E, C, D])
        WG = sb("WG", [P, E])
        bg = sb("bg", [1, E])
        b1r = sb("b1r", [E * C, P])
        b1 = sb("b1", [P, E * C])
        b2 = sb("b2", [E, D])
        K = sb("K", [P, NCONST])
        ones = sb("ones", [1, P])
        block_bf = sb("block_bf", [P, P], BF16)
        ident = K[:, IDENT:IDENT + P]

        def const(n):
            return K[:, n:n + 1]

        stats = sb("stats", [P, 2, J, 6])
        halves = sb("halves", [P, J, 2])
        apart = sb("apart", [P, J])
        spread = sb("spread", [P, J])
        squares = sb("squares", [P, J])
        mean = sb("mean", [P, 2, J])
        vare = sb("vare", [P, 2, J])
        rstd = sb("rstd", [P, 2, J])
        xnf = sb("xnf", [P, 2, J, D])
        xnT = sb("xnT", [P, 2, T])
        lg = sb("lg", [P, J, E])
        before = sb("before", [P, J, E, E])
        equal = sb("equal", [P, J, E, E])
        rank = sb("rank", [P, J, E])
        top = sb("top", [P, J])
        below = sb("below", [P, J, E])
        weight = sb("weight", [P, J, E])
        picked = sb("picked", [P, J, E])
        total = sb("total", [P, J])
        inv = sb("inv", [P, J])
        gate = sb("gate", [P, 2, J, E])
        gateT = sb("gateT", [E, 2, T])
        hid = sb("hid", [P, 2, C, T])
        xna = sb("xna", [P, 2, J, H, REP, HD])
        value = sb("value", [P, 2, J, H, W])
        negsum = sb("negsum", [P, 1])
        cent = sb("cent", [P, T])
        high = sb("high", [P, T], F16)
        square = sb("square", [P, T], BF16)
        keys = sb("keys", [P, T], F16)
        part = sb("part", [P, T], F16)
        key_even = sb("key_even", [P, 2, T], F16)
        key_odd = sb("key_odd", [P, 2, T], F16)
        query = sb("query", [P, 2, T], F16)
        RING = 4
        probs = sb("probs", [P, RING, 2, T])
        mixed = sb("mixed", [P, 2, T])
        recip = sb("recip", [P, J, Q])
        normed = sb("normed", [P, J, Q, HD])

        ps = ctx.enter_context(nc.psum_tensor("ps", [P, 8, T], F32))
        PREP, TURN = 6, 7

        names = """const_in weights x_first x_rest stored ones_set value_set block_set b1_turned b1_set
            f_halves f_apart f_mean f_spread f_squares f_vare f_rstd f_xn f_turned f_xnT f_logits f_lg f_before f_equal f_tied f_ranks f_rank f_top f_below
            f_weight f_sel f_picked f_total f_inv f_gate f_gturned f_gateT f_bias f_bias_added f_stats
            f_hidden f_relu_act f_relu_dve f_expert f_added
            a_stats a_halves a_apart a_mean a_spread a_squares a_vare a_rstd a_xn a_value a_turned a_sum a_cent a_high a_square a_norms a_keys a_part
            a_keyed a_query a_scores a_probs a_mixed a_copied a_back a_recip a_normed a_added""".split()
        sm = {n: sem(n) for n in names}

        block = ctx.enter_context(nc.Block())

        xs_in = x_in.rearrange("s (p j) d -> p s (j d)", j=J)
        xs_out = out.rearrange("s (p j) d -> p s (j d)", j=J)

        def tokens(s, j=0, n=J):
            return X[:, bass.ds((s * J + j) * D, n * D)]

        @block.sync
        def _(sp):
            sp.dma_start(X[:, 0:2 * J * D].rearrange("p (s c) -> p s c", s=2), xs_in[:, 0:2]).then_inc(sm["x_first"], 16)
            sp.dma_start(K[:, :], const_in).then_inc(sm["const_in"], 16)
            sp.dma_start(W1[:, :, :], w1_in.rearrange("e d f -> d e f")).then_inc(sm["weights"], 16)
            sp.dma_start(WG[:, :], wg_in).then_inc(sm["weights"], 16)
            sp.dma_start(bg[:, :], bg_in.rearrange("(a e) -> a e", a=1)).then_inc(sm["weights"], 16)
            sp.dma_start(b1r[:, :], b1_in.rearrange("e (c p) -> (e c) p", c=C)).then_inc(sm["weights"], 16)
            sp.dma_start(b2[:, :], b2_in).then_inc(sm["weights"], 16)
            sp.dma_start(W2[:, :, :, :], w2_in.rearrange("e (c p) d -> p e c d", c=C)).then_inc(sm["weights"], 16)
            sp.dma_start(X[:, 2 * J * D:].rearrange("p (s c) -> p s c", c=J * D), xs_in[:, 2:]).then_inc(sm["x_rest"], 16)

            def store(i):
                for u in range(2):
                    s = i * 2 + u
                    sp.wait_ge(sm["f_added"], ((S + s) * E) + E)
                    sp.dma_start(xs_out[:, bass.ds(s, 1)],
                                 tokens(s).rearrange("p (s c) -> p s c", s=1)).then_inc(sm["stored"], 16)
            pairs_of_sequences(sp, store)
            sp.wait_ge(sm["stored"], 16 * S)

        def norm_stats(dve, a, s, n, u):
            for j in range(J):
                nc.vector.bn_stats(stats[:, u, j, :], tokens(s, j, 1)).then_inc(sm[a + "stats"], 1)
            dve.wait_ge(sm[a + "stats"], n * J + J)
            even, odd = stats[:, u, :, 1:3], stats[:, u, :, 4:6]
            nc.vector.tensor_tensor(halves[:, :, :], even, odd, ALU.add).then_inc(sm[a + "halves"], 1)
            nc.vector.tensor_tensor(apart[:, :], even[:, :, 0], odd[:, :, 0], ALU.subtract).then_inc(sm[a + "apart"], 1)
            dve.wait_ge(sm[a + "halves"], n + 1)
            nc.vector.tensor_scalar(mean[:, u, :], halves[:, :, 0], 0.5, None, ALU.mult).then_inc(sm[a + "mean"], 1)
            dve.wait_ge(sm[a + "apart"], n + 1)
            nc.vector.scalar_tensor_tensor(spread[:, :], apart[:, :], D / 4.0, apart[:, :], ALU.mult, ALU.mult).then_inc(sm[a + "spread"], 1)
            dve.wait_ge(sm[a + "spread"], n + 1)
            nc.vector.tensor_tensor(squares[:, :], spread[:, :], halves[:, :, 1], ALU.add).then_inc(sm[a + "squares"], 1)
            dve.wait_ge(sm[a + "squares"], n + 1)
            nc.vector.tensor_scalar(vare[:, u, :], squares[:, :], 1.0 / D, EPS, ALU.mult, ALU.add).then_inc(sm[a + "vare"], 1)

        def norm_rows(dve, a, s, n, u, into, free):
            dve.wait_ge(sm[a + "mean"], n + 1)
            dve.wait_ge(sm[a + "rstd"], n + 1)
            for sem_name, count in free:
                reached(dve, sm[sem_name], count)
            for j in range(J):
                to, rows = into(tokens(s, j, 1), u, j)
                ins = nc.vector.tensor_scalar(to, rows, mean[:, u, j:j + 1], rstd[:, u, j:j + 1],
                                              ALU.subtract, ALU.mult)
            ins.then_inc(sm[a + "xn"], 1)

        def norm_pool(pool, a, n, u):
            pool.wait_ge(sm[a + "vare"], n + 1)
            nc.gpsimd.tensor_tensor(rstd[:, u, :], vare[:, u, :],
                                    const(MINUS_HALF).to_broadcast([P, J]), ALU.pow).then_inc(sm[a + "rstd"], 1)

        def ffn_tensor(pe, p):
            def turn(n, u):
                pe.wait_ge(sm["f_xn"], n + 1)
                reached(pe, sm["f_bias_added"], n)
                for j in range(J):
                    ins = nc.tensor.transpose(ps[:, PREP, j * P:(j + 1) * P], xnf[:, u, j, :], ident)
                ins.then_inc(sm["f_turned"], 1)

            def logits(n, u):
                pe.wait_ge(sm["f_xnT"], n + 1)
                reached(pe, sm["f_gateT"], n)
                for j in range(J):
                    o = ps[:, TURN, j * E:(j + 1) * E]
                    nc.tensor.matmul(o, xnT[:, u, j * P:(j + 1) * P], WG[:, :], start=True, stop=False)
                    ins = nc.tensor.matmul(o, ones[:, :], bg[:, :], start=False, stop=True)
                ins.then_inc(sm["f_logits"], 1)

            def turn_gates(n, u):
                pe.wait_ge(sm["f_gate"], n + 1)
                for j in range(J):
                    ins = nc.tensor.transpose(ps[0:E, TURN, j * P:(j + 1) * P], gate[:, u, j, :], ident)
                ins.then_inc(sm["f_gturned"], 1)

            def biases(n, u):
                pe.wait_ge(sm["f_gateT"], n + 1)
                for j in range(J):
                    ins = nc.tensor.matmul(ps[:, PREP, j * D:(j + 1) * D], gateT[:, u, j * P:(j + 1) * P], b2[:, :],
                                           start=True, stop=True)
                ins.then_inc(sm["f_bias"], 1)

            def hidden(n, u, e):
                if e == 0:
                    pe.wait_ge(sm["f_xnT"], n + 1)
                for c, done in enumerate(("f_relu_act", "f_relu_dve")):
                    reached(pe, sm[done], n * E + e - 1)
                    nc.tensor.matmul(ps[:, 2 * (e % 2) + c, :], W1[:, e, c * P:(c + 1) * P], xnT[:, u, :],
                                     start=True, stop=True).then_inc(sm["f_hidden"], 1)

            def expert(n, e):
                pe.wait_ge(sm["f_relu_act"], n * E + e + 1)
                pe.wait_ge(sm["f_relu_dve"], n * E + e + 1)
                reached(pe, sm["f_added"], n * E + e - 1)
                for j in range(J):
                    for c in range(C):
                        ins = nc.tensor.matmul(ps[:, 4 + e % 2, j * D:(j + 1) * D], hid[:, e % 2, c, j * P:(j + 1) * P],
                                               W2[:, e, c, :], start=(c == 0), stop=(c == C - 1))
                ins.then_inc(sm["f_expert"], 1)

            def prepare(n, u):
                turn(n, u)
                logits(n, u)
                turn_gates(n, u)

            def body(i):
                for u in range(2):
                    n = i * 2 + u + p * S
                    last = isinstance(i, int) and i * 2 + u == S - 1
                    for e in range(E):
                        if not last:
                            if e == 3:
                                turn(n + 1, 1 - u)
                            if e == 5:
                                logits(n + 1, 1 - u)
                        if e < E - 1:
                            hidden(n, u, e + 1)
                        elif not last:
                            hidden(n + 1, 1 - u, 0)
                        expert(n, e)
                        if e == 0:
                            biases(n, u)
                        if e == 7 and not last:
                            turn_gates(n + 1, 1 - u)

            prepare(p * S, 0)
            hidden(p * S, 0, 0)
            pairs_of_sequences(pe, body)

        def ffn_vector(dve, p):
            def ranking(n):
                dve.wait_ge(sm["f_logits"], n + 1)
                nc.vector.tensor_copy(lg[:, :, :], ps[:, TURN, 0:J * E].rearrange("p (j e) -> p j e", e=E)).then_inc(sm["f_lg"], 1)
                dve.wait_ge(sm["f_lg"], n + 1)
                other = lg[:, :, :].unsqueeze(2).to_broadcast([P, J, E, E])
                own = lg[:, :, :].unsqueeze(3).to_broadcast([P, J, E, E])
                tri = K[:, TRI:TRI + E * E].unsqueeze(1).to_broadcast([P, J, E * E])
                nc.vector.tensor_tensor(equal[:, :, :, :], other, own, ALU.is_equal).then_inc(sm["f_equal"], 1)
                nc.vector.tensor_tensor(before[:, :, :, :], other, own, ALU.is_gt).then_inc(sm["f_before"], 1)
                nc.vector.tensor_reduce(top[:, :], lg[:, :, :], AX.X, ALU.max).then_inc(sm["f_top"], 1)
                dve.wait_ge(sm["f_equal"], n + 1)
                flat = equal[:, :, :, :].rearrange("p j e f -> p j (e f)")
                nc.vector.tensor_tensor(flat, flat, tri, ALU.mult).then_inc(sm["f_tied"], 1)
                dve.wait_ge(sm["f_top"], n + 1)
                nc.vector.tensor_tensor(below[:, :, :], lg[:, :, :], top[:, :].unsqueeze(2).to_broadcast([P, J, E]),
                                        ALU.subtract).then_inc(sm["f_below"], 1)
                dve.wait_ge(sm["f_tied"], n + 1)
                dve.wait_ge(sm["f_before"], n + 1)
                nc.vector.tensor_tensor(before[:, :, :, :], before[:, :, :, :], equal[:, :, :, :], ALU.add).then_inc(sm["f_ranks"], 1)
                dve.wait_ge(sm["f_ranks"], n + 1)
                nc.vector.tensor_reduce(rank[:, :, :], before[:, :, :, :], AX.X, ALU.add).then_inc(sm["f_rank"], 1)

            def gating(n, u):
                dve.wait_ge(sm["f_rank"], n + 1)
                dve.wait_ge(sm["f_weight"], n + 1)
                nc.vector.scalar_tensor_tensor(picked[:, :, :], rank[:, :, :], TOPK - 0.5, weight[:, :, :],
                                               ALU.is_lt, ALU.mult).then_inc(sm["f_picked"], 1)
                dve.wait_ge(sm["f_picked"], n + 1)
                nc.vector.tensor_reduce(total[:, :], picked[:, :, :], AX.X, ALU.add).then_inc(sm["f_total"], 1)
                dve.wait_ge(sm["f_total"], n + 1)
                nc.vector.reciprocal(inv[:, :], total[:, :]).then_inc(sm["f_inv"], 1)
                dve.wait_ge(sm["f_inv"], n + 1)
                nc.vector.scalar_tensor_tensor(gate[:, u, :, :], picked[:, :, :], 0.5,
                                               inv[:, :].unsqueeze(2).to_broadcast([P, J, E]), ALU.mult, ALU.mult).then_inc(sm["f_gate"], 1)

            def add_bias(s, n):
                dve.wait_ge(sm["f_bias"], n + 1)
                dve.wait_ge(sm["f_added"], n * E + 1)
                nc.vector.tensor_tensor(tokens(s), tokens(s), ps[:, PREP, :], ALU.add).then_inc(sm["f_bias_added"], 1)

            def relu(n, e):
                dve.wait_ge(sm["f_hidden"], (n * E + e) * C + 2)
                reached(dve, sm["f_expert"], n * E + e - 1)
                nc.vector.tensor_scalar(hid[:, e % 2, 1, :], ps[:, 2 * (e % 2) + 1, :], b1[:, e * C + 1:e * C + 2], 0.0,
                                        ALU.add, ALU.max).then_inc(sm["f_relu_dve"], 1)

            def add_expert(s, n, u, e):
                dve.wait_ge(sm["f_expert"], n * E + e + 1)
                if e == 1:
                    dve.wait_ge(sm["f_bias_added"], n + 1)
                elif e > 1:
                    dve.wait_ge(sm["f_added"], n * E + e)
                for j in range(J):
                    ins = nc.vector.scalar_tensor_tensor(tokens(s, j, 1), ps[:, 4 + e % 2, j * D:(j + 1) * D],
                                                         gate[:, u, j, e:e + 1], tokens(s, j, 1), ALU.mult, ALU.add)
                ins.then_inc(sm["f_added"], 1)

            def rows(s, n, u):
                norm_rows(dve, "f_", s, n, u, lambda rows, u, j: (xnf[:, u, j, :], rows), [("f_turned", n - 1)])

            def body(i):
                for u in range(2):
                    s = i * 2 + u
                    n = s + p * S
                    last = isinstance(i, int) and s == S - 1
                    for e in range(E):
                        if e < E - 1:
                            relu(n, e + 1)
                        elif not last:
                            relu(n + 1, 0)
                        add_expert(s, n, u, e)
                        if e == 0:
                            add_bias(s, n)
                        if not last:
                            if e == 0:
                                if p == 0 and isinstance(i, int) and s == 1:
                                    dve.wait_ge(sm["x_rest"], 16)
                                norm_stats(dve, "f_", s + 1, n + 1, 1 - u)
                            if e == 1:
                                rows(s + 1, n + 1, 1 - u)
                            if e == 5:
                                ranking(n + 1)
                            if e == 6:
                                gating(n + 1, 1 - u)

            if p == 1:
                dve.wait_ge(sm["a_added"], S * G)
            norm_stats(dve, "f_", 0, p * S, 0)
            rows(0, p * S, 0)
            ranking(p * S)
            gating(p * S, 0)
            relu(p * S, 0)
            pairs_of_sequences(dve, body)

        def ffn_scalar(act, p):
            def rows(n, u):
                act.wait_ge(sm["f_turned"], n + 1)
                reached(act, sm["f_hidden"], (n - 1) * E * C)
                nc.scalar.activation(xnT[:, u, :], ps[:, PREP, :], ACT.Copy).then_inc(sm["f_xnT"], 1)

            def weights(n):
                act.wait_ge(sm["f_below"], n + 1)
                reached(act, sm["f_picked"], n)
                nc.scalar.activation(weight[:, :, :], below[:, :, :], ACT.Exp).then_inc(sm["f_weight"], 1)

            def gates(n, u):
                act.wait_ge(sm["f_gturned"], n + 1)
                reached(act, sm["f_bias"], n - 1)
                nc.scalar.activation(gateT[:, u, :], ps[0:E, TURN, :], ACT.Copy).then_inc(sm["f_gateT"], 1)

            def relu(n, e):
                act.wait_ge(sm["f_hidden"], (n * E + e) * C + 1)
                reached(act, sm["f_expert"], n * E + e - 1)
                nc.scalar.activation(hid[:, e % 2, 0, :], ps[:, 2 * (e % 2), :], ACT.Relu,
                                     bias=b1[:, e * C:e * C + 1]).then_inc(sm["f_relu_act"], 1)

            def body(i):
                for u in range(2):
                    n = i * 2 + u + p * S
                    last = isinstance(i, int) and i * 2 + u == S - 1
                    for e in range(E):
                        if not last:
                            if e == 4:
                                rows(n + 1, 1 - u)
                        if e < E - 1:
                            relu(n, e + 1)
                        elif not last:
                            relu(n + 1, 0)
                        if not last and e == 6:
                            weights(n + 1)
                        if not last and e == 7:
                            gates(n + 1, 1 - u)

            rows(p * S, 0)
            weights(p * S)
            gates(p * S, 0)
            relu(p * S, 0)
            pairs_of_sequences(act, body)

        def ffn_gpsimd(pool, p):
            def body(i):
                for u in range(2):
                    if not (isinstance(i, int) and i * 2 + u == S - 1):
                        norm_pool(pool, "f_", i * 2 + u + 1 + p * S, 1 - u)
            norm_pool(pool, "f_", p * S, 0)
            pairs_of_sequences(pool, body)

        STAGES = J * 2

        def attn_tensor(pe):
            def turn(g, s, u, hg):
                if hg == 0:
                    pe.wait_ge(sm["a_xn"], s + 1)
                reached(pe, sm["a_query"], g)
                for j in range(J):
                    rows = xna[:, u, j, hg * Q:(hg + 1) * Q, :, :].rearrange("p q r i -> p (q r i)")
                    ins = nc.tensor.transpose(ps[:, PREP, j * P:(j + 1) * P], rows, ident)
                ins.then_inc(sm["a_turned"], 1)

            def norms(g):
                pe.wait_ge(sm["a_square"], g + 1)
                nc.tensor.matmul(ps[:, PREP, :], block_bf[:, :], square[:, :], start=True, stop=True).then_inc(sm["a_norms"], 1)

            def scores(g, b, kk):
                j, half = kk // 2, kk % 2
                if kk == 0:
                    pe.wait_ge(sm["a_query"], g + 1)
                reached(pe, sm["a_probs"], g * STAGES + kk - 1)
                at = slice(half * 2 * W, (half + 1) * 2 * W)
                for odd, keyed in enumerate((key_even, key_odd)):
                    ins = nc.tensor.matmul(ps[:, 2 * (kk % 2) + odd, :], keyed[at, b, j * P:(j + 1) * P], query[at, b, :],
                                           start=True, stop=True)
                ins.then_inc(sm["a_scores"], 1)

            def mix(g, s, u, b, hg, kk):
                j, half = kk // 2, kk % 2
                if kk == 0:
                    pe.wait_ge(sm["a_value"], s + 1)
                    reached(pe, sm["a_copied"], g - 1)
                pe.wait_ge(sm["a_probs"], g * STAGES + kk + 1)
                for odd in range(2):
                    q = 2 * half + odd
                    ins = nc.tensor.matmul(ps[q * W:(q + 1) * W, 4 + b, :], value[:, u, j, hg * Q + q, :],
                                           probs[:, kk % RING, odd, :], start=(j == 0), stop=(j == J - 1))
                ins.then_inc(sm["a_mixed"], 1)

            def back(g, b):
                pe.wait_ge(sm["a_copied"], g + 1)
                reached(pe, sm["a_normed"], g)
                for j in range(J):
                    ins = nc.tensor.transpose(ps[:, TURN, j * P:(j + 1) * P], mixed[:, b, j * P:(j + 1) * P], ident)
                ins.then_inc(sm["a_back"], 1)

            def body(i):
                for t in range(2 * G):
                    g, u, hg, b = i * 2 * G + t, t // G, t % G, t % 2
                    first = isinstance(i, int) and i * 2 * G + t == 0
                    last = isinstance(i, int) and i * 2 * G + t == S * G - 1
                    for kk in range(STAGES):
                        if kk < STAGES - 2:
                            scores(g, b, kk + 2)
                        elif not last:
                            scores(g + 1, 1 - b, kk + 2 - STAGES)
                        mix(g, i * 2 + u, u, b, hg, kk)
                        if kk == 3 and not last:
                            norms(g + 1)
                        if kk == 4 and not first:
                            back(g - 1, 1 - b)
                        if kk == 7 and not last and not (isinstance(i, int) and i * 2 * G + t == S * G - 2):
                            turn(g + 2, i * 2 + (t + 2) // G, (t + 2) // G % 2, (t + 2) % G)

            pe.wait_ge(sm["f_relu_act"], S * E)
            pe.wait_ge(sm["f_relu_dve"], S * E)
            pe.wait_ge(sm["f_added"], S * E)
            pe.wait_ge(sm["f_bias_added"], S)
            turn(0, 0, 0, 0)
            norms(0)
            turn(1, 0, 0, 1)
            scores(0, 0, 0)
            scores(0, 0, 1)
            pairs_of_sequences(pe, body)
            back(S * G - 1, 1)

        def attn_vector(dve):
            def centre(g):
                dve.wait_ge(sm["a_turned"], g + 1)
                nc.vector.reduce_sum(negsum[:, :], ps[:, PREP, :], AX.X, negate=True).then_inc(sm["a_sum"], 1)
                dve.wait_ge(sm["a_sum"], g + 1)
                reached(dve, sm["a_square"], g)
                nc.vector.tensor_scalar(cent[:, :], ps[:, PREP, :], CENTRED, negsum[:, :], ALU.mult, ALU.add).then_inc(sm["a_cent"], 1)

            def operands(g, b):
                dve.wait_ge(sm["a_cent"], g + 1)
                nc.vector.tensor_copy(high[:, :], cent[:, :]).then_inc(sm["a_high"], 1)
                dve.wait_ge(sm["a_high"], g + 1)
                nc.vector.scalar_tensor_tensor(keys[:, :], high[:, :], const(KEY_LO), cent[:, :],
                                               ALU.mult, ALU.add).then_inc(sm["a_keys"], 1)
                nc.vector.scalar_tensor_tensor(part[:, :], high[:, :], const(QUERY_LO), cent[:, :],
                                               ALU.mult, ALU.add).then_inc(sm["a_part"], 1)
                dve.wait_ge(sm["a_keys"], g + 1)
                reached(dve, sm["a_scores"], (g - 1) * STAGES)
                nc.vector.tensor_scalar(key_even[:, b, :], keys[:, :], const(KEEP_EVEN), const(UNIT_EVEN), ALU.mult, ALU.add)
                nc.vector.tensor_scalar(key_odd[:, b, :], keys[:, :], const(KEEP_ODD), const(UNIT_ODD), ALU.mult, ALU.add).then_inc(sm["a_keyed"], 1)
                dve.wait_ge(sm["a_part"], g + 1)
                dve.wait_ge(sm["a_norms"], g + 1)
                nc.vector.scalar_tensor_tensor(query[:, b, :], ps[:, PREP, :], const(SHIFT_ROW), part[:, :],
                                               ALU.mult, ALU.add).then_inc(sm["a_query"], 1)

            def copy(g, b):
                dve.wait_ge(sm["a_mixed"], g * STAGES + STAGES)
                reached(dve, sm["a_back"], g - 1)
                nc.vector.tensor_copy(mixed[:, b, :], ps[:, 4 + b, :]).then_inc(sm["a_copied"], 1)

            def finish(g, s, hg):
                dve.wait_ge(sm["a_back"], g + 1)
                back = ps[:, TURN, :].rearrange("p (j q w) -> p j q w", j=J, q=Q)
                nc.vector.reciprocal(recip[:, :, :], back[:, :, :, HD]).then_inc(sm["a_recip"], 1)
                dve.wait_ge(sm["a_recip"], g + 1)
                nc.vector.tensor_tensor(normed[:, :, :, :], back[:, :, :, 0:HD],
                                        recip[:, :, :].unsqueeze(3).to_broadcast([P, J, Q, HD]), ALU.mult).then_inc(sm["a_normed"], 1)
                dve.wait_ge(sm["a_normed"], g + 1)
                rows = tokens(s).rearrange("p (j d) -> p j d", j=J)[:, :, hg * Q * HD:(hg + 1) * Q * HD]
                nc.vector.tensor_tensor(rows, rows, normed[:, :, :, :].rearrange("p j q i -> p j (q i)"),
                                        ALU.add).then_inc(sm["a_added"], 1)

            def rows(s, u):
                def copies(rows, u, j):
                    rows = rows.rearrange("p (h i) -> p h i", i=HD).unsqueeze(2).to_broadcast([P, H, REP, HD])
                    return xna[:, u, j, :, :, :], rows
                norm_rows(dve, "a_", s, s, u, copies, [("a_turned", (s - 1) * G), ("a_value", s - 1)])

            def body(i):
                for t in range(2 * G):
                    g, s, u, hg, b = i * 2 * G + t, i * 2 + t // G, t // G, t % G, t % 2
                    first = isinstance(i, int) and i * 2 * G + t == 0
                    last = isinstance(i, int) and i * 2 * G + t == S * G - 1
                    if not last:
                        centre(g + 1)
                    if not first:
                        copy(g - 1, 1 - b)
                    if not last:
                        operands(g + 1, 1 - b)
                    if not first:
                        finish(g - 1, i * 2 + (t - 1) // G, (t - 1) % G)
                    if not (isinstance(i, int) and s == S - 1):
                        if hg == 0:
                            norm_stats(dve, "a_", s + 1, s + 1, 1 - u)
                        if hg == 1:
                            rows(s + 1, 1 - u)

            dve.wait_ge(sm["f_added"], S * E)
            norm_stats(dve, "a_", 0, 0, 0)
            rows(0, 0)
            centre(0)
            operands(0, 0)
            pairs_of_sequences(dve, body)
            copy(S * G - 1, 1)
            finish(S * G - 1, S - 1, G - 1)

        def attn_scalar(act):
            def body(i):
                for t in range(2 * G):
                    g = i * 2 * G + t
                    for kk in range(STAGES):
                        act.wait_ge(sm["a_scores"], g * STAGES + kk + 1)
                        reached(act, sm["a_mixed"], g * STAGES + kk - RING + 1)
                        nc.scalar.activation(probs[:, kk % RING, :, :], ps[:, 2 * (kk % 2):2 * (kk % 2) + 2, :], ACT.Exp,
                                             bias=const(MINUS_SHIFT), scale=SCORE).then_inc(sm["a_probs"], 1)
            pairs_of_sequences(act, body)

        def attn_gpsimd(pool):
            def square_rows(g):
                pool.wait_ge(sm["a_cent"], g + 1)
                reached(pool, sm["a_norms"], g)
                nc.gpsimd.tensor_tensor(square[:, :], cent[:, :], cent[:, :], ALU.mult).then_inc(sm["a_square"], 1)

            def values_due(s):
                pool.wait_ge(sm["a_xn"], s + 1)
                reached(pool, sm["a_mixed"], (s - 1) * G * STAGES)

            def values(u):
                for j in range(J):
                    ins = nc.gpsimd.tensor_copy(value[:, u, j, :, 0:HD], xna[:, u, j, :, 0, :])
                ins.then_inc(sm["a_value"], 1)

            def body(i):
                for t in range(2 * G):
                    g, s, u, hg = i * 2 * G + t, i * 2 + t // G, t // G, t % G
                    more = not (isinstance(i, int) and s == S - 1)
                    if hg == 2 and more:
                        values_due(s + 1)
                    if not (isinstance(i, int) and i * 2 * G + t == S * G - 1):
                        square_rows(g + 1)
                    if hg == 0 and more:
                        norm_pool(pool, "a_", s + 1, 1 - u)
                    if hg == 2 and more:
                        values(1 - u)

            norm_pool(pool, "a_", 0, 0)
            values_due(0)
            square_rows(0)
            values(0)
            pairs_of_sequences(pool, body)

        @block.gpsimd
        def _(pool):
            nc.gpsimd.memset(ones[:, :], 1.0).then_inc(sm["ones_set"], 1)
            nc.gpsimd.memset(value[:, :, :, :, :], 0.0).then_inc(sm["value_set"], 1)
            pool.wait_ge(sm["value_set"], 1)
            nc.gpsimd.memset(value[:, :, :, :, HD:HD + 1], 1.0).then_inc(sm["value_set"], 1)
            pool.wait_ge(sm["value_set"], 2)
            pool.wait_ge(sm["const_in"], 16)
            ffn_gpsimd(pool, 0)
            attn_gpsimd(pool)
            ffn_gpsimd(pool, 1)

        @block.tensor
        def _(pe):
            pe.wait_ge(sm["const_in"], 16)
            pe.wait_ge(sm["weights"], 16 * 6)
            nc.tensor.transpose(ps[:, TURN, 0:E * C], b1r[:, :], ident[0:E * C, 0:E * C]).then_inc(sm["b1_turned"], 1)
            pe.wait_ge(sm["b1_set"], 1)
            pe.wait_ge(sm["block_set"], 1)
            pe.wait_ge(sm["ones_set"], 1)
            ffn_tensor(pe, 0)
            attn_tensor(pe)
            pe.wait_ge(sm["a_probs"], S * G * STAGES)
            pe.wait_ge(sm["a_added"], S * G)
            ffn_tensor(pe, 1)

        @block.scalar
        def _(act):
            act.wait_ge(sm["b1_turned"], 1)
            nc.scalar.activation(b1[:, :], ps[:, TURN, 0:E * C], ACT.Copy).then_inc(sm["b1_set"], 1)
            act.wait_ge(sm["b1_set"], 1)
            ffn_scalar(act, 0)
            attn_scalar(act)
            ffn_scalar(act, 1)

        @block.vector
        def _(dve):
            dve.wait_ge(sm["const_in"], 16)
            nc.vector.tensor_copy(block_bf[:, :], K[:, BLOCK:BLOCK + P]).then_inc(sm["block_set"], 1)
            dve.wait_ge(sm["x_first"], 16)
            ffn_vector(dve, 0)
            attn_vector(dve)
            ffn_vector(dve, 1)


def kernel(**inputs):
    import concourse.bacc as bacc
    from concourse.bass_utils import run_bass_kernel_spmd as run

    nc = bacc.Bacc("TRN2", target_bir_lowering=False, num_devices=1)
    names = ["L0_attn_x", "L0_ffn_Wg", "L0_ffn_bg", "L0_ffn_W1", "L0_ffn_b1", "L0_ffn_W2", "L0_ffn_b2"]
    arrays = {"in_" + n: np.ascontiguousarray(inputs[n]) for n in names}
    arrays["in_constants"] = constants()
    args = [nc.dram_tensor(n, a.shape, F32, kind="ExternalInput").ap() for n, a in arrays.items()]
    out = nc.dram_tensor("out", (S, T, D), F32, kind="ExternalOutput").ap()
    build(nc, *args, out)
    return run(nc, [arrays], core_ids=[0]).results[0]["out"]
```

```python
from contextlib import ExitStack

import concourse.bass as bass
import numpy as np
from concourse import mybir

P = 128
S, T, D = 16, 512, 128
J = T // P
E, F = 8, 256
C = F // P
TOPK = 2
PARTS = 4
AHEAD = 2
H, HD = 16, 8
Q = 4
G = H // Q
W = P // Q
STAGES = J * 2
REP = W // HD
EPS = 1e-5
CENTRED = float(T)
SCORE = 1.0 / CENTRED ** 2
UNIT_ROWS = 4096.0
SHIFT = 50.0

F32, F16, BF16 = mybir.dt.float32, mybir.dt.float16, mybir.dt.bfloat16
F32R = mybir.dt.float32r
ALU = mybir.AluOpType
ACT = mybir.ActivationFunctionType
AX = mybir.AxisListType

IDENT, BLOCK, TRI = 0, P, 2 * P
KEY_LO, QUERY_LO, SHIFT_ROW, KEEP_EVEN, UNIT_EVEN, KEEP_ODD, UNIT_ODD, MINUS_HALF, MINUS_SHIFT, B2_HIGH, B2_LOW = range(
    TRI + E * E, TRI + E * E + 11)
NCONST = TRI + E * E + 11


def constants():
    c = np.zeros((P, NCONST), np.float32)
    row = np.arange(P)
    quadrant, copy = row // W, row % W // HD
    c[:, IDENT:IDENT + P] = np.eye(P)
    c[:, BLOCK:BLOCK + P] = (quadrant[:, None] == quadrant[None, :]) & (copy == 0)[:, None]
    c[:, TRI:TRI + E * E] = (np.arange(E)[None, :] < np.arange(E)[:, None]).reshape(-1)
    c[:, KEY_LO] = -1.0 * (copy == 1)
    c[:, QUERY_LO] = -1.0 * (copy >= 2)
    c[:, SHIFT_ROW] = -1.0 / (UNIT_ROWS * HD) * (copy == 3)
    for odd, keep, unit in ((0, KEEP_EVEN, UNIT_EVEN), (1, KEEP_ODD, UNIT_ODD)):
        c[:, keep] = (quadrant % 2 == odd) & (copy < 3)
        c[:, unit] = UNIT_ROWS * ((quadrant % 2 == odd) & (copy == 3))
    c[:, MINUS_HALF] = -0.5
    c[:, MINUS_SHIFT] = -SHIFT
    c[:, B2_HIGH] = (E <= row) & (row < 3 * E)
    c[:, B2_LOW] = (3 * E <= row) & (row < 4 * E)
    return c


def reached(eng, sem, value):
    if not isinstance(value, int) or value > 0:
        eng.wait_ge(sem, value)


def pairs_of_sequences(eng, body):
    n = S // 2
    body(0)
    with eng.Fori(1, n - 1) as i:
        body(i)
    body(n - 1)


def build(nc, x_in, wg_in, bg_in, w1_in, b1_in, w2_in, b2_in, const_in, gates_dram, out):
    with ExitStack() as ctx:
        def sb(name, shape, dt=F32):
            return ctx.enter_context(nc.sbuf_tensor(name, shape, dt))

        def sem(name):
            return ctx.enter_context(nc.semaphore(name))

        X = sb("X", [P, S * J * D])
        W1 = sb("W1", [P, E, F])
        W1h, W1l = sb("W1h", [P, E, F], F32R), sb("W1l", [P, E, F], F32R)
        W2h, W2l = sb("W2h", [P, E, C, D], F32R), sb("W2l", [P, E, C, D], F32R)
        WG = sb("WG", [P, E])
        bg = sb("bg", [P, E])
        b1r = sb("b1r", [E * C, P])
        b1 = sb("b1", [P, E * C])
        b2 = sb("b2", [PARTS * E, D])
        b2_high = sb("b2_high", [PARTS * E, D], F32R)
        b2_low = sb("b2_low", [PARTS * E, D])
        b2p = sb("b2p", [PARTS * E, D], F32R)
        K = sb("K", [P, NCONST])
        block_bf = sb("block_bf", [P, P], BF16)
        ident = K[:, IDENT:IDENT + P]

        def const(n):
            return K[:, n:n + 1]

        stats = sb("stats", [P, 2, J, 6])
        halves = sb("halves", [P, J, 2])
        apart = sb("apart", [P, J])
        spread = sb("spread", [P, J])
        squares = sb("squares", [P, J])
        mean = sb("mean", [P, 2, J])
        vare = sb("vare", [P, 2, J])
        rstd = sb("rstd", [P, 2, J])
        xnf = sb("xnf", [P, 2, J, D])
        xnT = sb("xnT", [P, T])
        xh, xl = sb("xh", [P, 2, T], F32R), sb("xl", [P, 2, T], F32R)
        lg = sb("lg", [P, J, E])
        before = sb("before", [P, J, E, E])
        equal = sb("equal", [P, J, E, E])
        tied = sb("tied", [P, J, E, E])
        ranks = sb("ranks", [P, J, E, E])
        rank = sb("rank", [P, J, E])
        top = sb("top", [P, J])
        below = sb("below", [P, J, E])
        weight = sb("weight", [P, J, E])
        picked = sb("picked", [P, J, E])
        total = sb("total", [P, J])
        inv = sb("inv", [P, J])
        gate_parts = sb("gate_parts", [P, J, PARTS, E])
        gateT = sb("gateT", [PARTS * E, 2, T], F32R)
        gate_rows = sb("gate_rows", [E, 2, T])
        hid = sb("hid", [P, 2, C, T])
        gated = sb("gated", [P, 2, C, T])
        gh, gl = sb("gh", [P, 2, C, T], F32R), sb("gl", [P, 2, C, T], F32R)
        yT = sb("yT", [P, T])
        xna = sb("xna", [P, 2, J, H, REP, HD])
        value = sb("value", [P, 2, J, H, W])
        negsum = sb("negsum", [P, 1])
        cent = sb("cent", [P, T])
        high = sb("high", [P, T], F16)
        square = sb("square", [P, T], BF16)
        keys = sb("keys", [P, T], F16)
        part = sb("part", [P, T], F16)
        key_even = sb("key_even", [P, 2, T], F16)
        key_odd = sb("key_odd", [P, 2, T], F16)
        query = sb("query", [P, 2, T], F16)
        RING = 4
        probs = sb("probs", [P, RING, 2, T])
        mixed = sb("mixed", [P, 2, T])
        gates_on_all = [probs[:, :, :, :].rearrange("p r o t -> p (r o t)").rearrange("p (e t) -> p e t", e=E),
                        xna[:, :, :, :, :, :].rearrange("p u j h r i -> p (u j h r i)").rearrange("p (e t) -> p e t", e=E)]
        W2 = xna[:, 0, :, :, :, :].rearrange("p j h r i -> p (j h r i)").rearrange("p (e c d) -> p e c d", e=E, c=C)
        recip = sb("recip", [P, J, Q])
        normed = sb("normed", [P, J, Q, HD])

        ps = ctx.enter_context(nc.psum_tensor("ps", [P, 8, T], F32))
        OUTPUT, BACK = 4, 5
        PREP, TURN = 6, 7

        names = """const_in w1_in w2_in small_in x_first x_rest stored value_set block_set b1_turned b1_set
            w1_high w1_low w2_high w2_low b2_high_set b2_low_set b2_scaled b2_set
            f_halves f_apart f_mean f_spread f_squares f_vare f_rstd f_xn f_turned f_xnT f_xh f_xl f_logits f_lg f_before
            f_equal f_tied f_ranks f_rank f_top f_below f_weight f_picked f_total f_inv f_gate f_gate_high
            f_parts f_gturned f_gateT f_gate_rows f_gates_stored f_gates_ahead f_gates_rest
            f_stats f_hidden f_relu f_gated f_high f_low_dve f_low_pool f_expert
            f_output f_back f_added
            a_stats a_halves a_apart a_mean a_spread a_squares a_vare a_rstd a_xn a_value a_turned a_sum a_cent a_high a_square a_norms a_keys a_part
            a_keyed a_query a_scores a_probs a_mixed a_copied a_back a_recip a_normed a_added""".split()
        sm = {n: sem(n) for n in names}

        block = ctx.enter_context(nc.Block())

        xs_in = x_in.rearrange("s (p j) d -> p s (j d)", j=J)
        xs_out = out.rearrange("s (p j) d -> p s (j d)", j=J)

        def tokens(s, j=0, n=J):
            return X[:, bass.ds((s * J + j) * D, n * D)]

        @block.sync
        def _(sp):
            sp.dma_start(X[:, 0:2 * J * D].rearrange("p (s c) -> p s c", s=2), xs_in[:, 0:2]).then_inc(sm["x_first"], 16)
            sp.dma_start(WG[:, :], wg_in).then_inc(sm["small_in"], 16)
            sp.dma_start(bg[:, :], bg_in.rearrange("(a e) -> a e", a=1).to_broadcast([P, E])).then_inc(sm["small_in"], 16)
            sp.dma_start(b1r[:, :], b1_in.rearrange("e (c p) -> (e c) p", c=C)).then_inc(sm["small_in"], 16)
            for k in range(PARTS):
                sp.dma_start(b2[k * E:(k + 1) * E, :], b2_in).then_inc(sm["small_in"], 16)
            sp.dma_start(X[:, 2 * J * D:].rearrange("p (s c) -> p s c", c=J * D), xs_in[:, 2:]).then_inc(sm["x_rest"], 16)

            def spread_gates(n, u):
                sp.wait_ge(sm["f_gate_rows"], n + 1)
                sp.dma_start(gates_dram[u], gate_rows[:, u, :]).then_inc(sm["f_gates_stored"], 16)
                sp.wait_ge(sm["f_gates_stored"], 16 * (n + 1))
                for done, experts in (("f_gates_ahead", slice(0, AHEAD)), ("f_gates_rest", slice(AHEAD, E))):
                    sp.dma_start(gates_on_all[u][:, experts, :], gates_dram[u:u + 1, experts, :].to_broadcast(
                        [P, experts.stop - experts.start, T])).then_inc(sm[done], 16)

            def store(s):
                sp.wait_ge(sm["f_added"], S + s + 1)
                sp.dma_start(xs_out[:, bass.ds(s, 1)],
                             tokens(s).rearrange("p (s c) -> p s c", s=1)).then_inc(sm["stored"], 16)

            for p in range(2):
                def body(i):
                    for u in range(2):
                        s = i * 2 + u
                        if p == 1 and not (isinstance(i, int) and s == 0):
                            store(s - 1)
                        if not (isinstance(i, int) and s == S - 1):
                            if p == 0 and isinstance(i, int) and s == 0:
                                sp.wait_ge(sm["w2_low"], 1)
                            spread_gates(p * S + s + 1, 1 - u)

                if p == 1:
                    sp.wait_ge(sm["a_mixed"], S * G * STAGES)
                    sp.wait_ge(sm["a_turned"], S * G)
                    sp.wait_ge(sm["a_value"], S)
                spread_gates(p * S, 0)
                pairs_of_sequences(sp, body)
            store(S - 1)
            sp.wait_ge(sm["stored"], 16 * S)

        def norm_stats(dve, a, s, n, u):
            for j in range(J):
                nc.vector.bn_stats(stats[:, u, j, :], tokens(s, j, 1)).then_inc(sm[a + "stats"], 1)

        def norm_sums(dve, a, n, u):
            dve.wait_ge(sm[a + "stats"], n * J + J)
            even, odd = stats[:, u, :, 1:3], stats[:, u, :, 4:6]
            nc.vector.tensor_tensor(halves[:, :, :], even, odd, ALU.add).then_inc(sm[a + "halves"], 1)
            nc.vector.tensor_tensor(apart[:, :], even[:, :, 0], odd[:, :, 0], ALU.subtract).then_inc(sm[a + "apart"], 1)
            dve.wait_ge(sm[a + "halves"], n + 1)
            nc.vector.tensor_scalar(mean[:, u, :], halves[:, :, 0], 0.5, None, ALU.mult).then_inc(sm[a + "mean"], 1)
            dve.wait_ge(sm[a + "apart"], n + 1)
            nc.vector.scalar_tensor_tensor(spread[:, :], apart[:, :], D / 4.0, apart[:, :], ALU.mult, ALU.mult).then_inc(sm[a + "spread"], 1)
            dve.wait_ge(sm[a + "spread"], n + 1)
            nc.vector.tensor_tensor(squares[:, :], spread[:, :], halves[:, :, 1], ALU.add).then_inc(sm[a + "squares"], 1)
            dve.wait_ge(sm[a + "squares"], n + 1)
            nc.vector.tensor_scalar(vare[:, u, :], squares[:, :], 1.0 / D, EPS, ALU.mult, ALU.add).then_inc(sm[a + "vare"], 1)

        def norm_rows(dve, a, s, n, u, into, free):
            dve.wait_ge(sm[a + "mean"], n + 1)
            dve.wait_ge(sm[a + "rstd"], n + 1)
            for sem_name, count in free:
                reached(dve, sm[sem_name], count)
            for j in range(J):
                to, rows = into(tokens(s, j, 1), u, j)
                ins = nc.vector.tensor_scalar(to, rows, mean[:, u, j:j + 1], rstd[:, u, j:j + 1],
                                              ALU.subtract, ALU.mult)
            ins.then_inc(sm[a + "xn"], 1)

        def norm_pool(pool, a, n, u):
            pool.wait_ge(sm[a + "vare"], n + 1)
            nc.gpsimd.tensor_tensor(rstd[:, u, :], vare[:, u, :],
                                    const(MINUS_HALF).to_broadcast([P, J]), ALU.pow).then_inc(sm[a + "rstd"], 1)

        def ffn_tensor(pe, p):
            def turn(n, u):
                pe.wait_ge(sm["f_xn"], n + 1)
                reached(pe, sm["f_xl"], n)
                for j in range(J):
                    ins = nc.tensor.transpose(ps[:, PREP, j * P:(j + 1) * P], xnf[:, u, j, :], ident)
                ins.then_inc(sm["f_turned"], 1)

            def logits(n):
                pe.wait_ge(sm["f_xnT"], n + 1)
                reached(pe, sm["f_gate_rows"], n)
                for j in range(J):
                    ins = nc.tensor.matmul(ps[:, TURN, j * E:(j + 1) * E], xnT[:, j * P:(j + 1) * P], WG[:, :],
                                           start=True, stop=True)
                ins.then_inc(sm["f_logits"], 1)

            def turn_gates(n):
                pe.wait_ge(sm["f_parts"], n + 1)
                for j in range(J):
                    ins = nc.tensor.transpose(ps[0:PARTS * E, TURN, j * P:(j + 1) * P],
                                              gate_parts[:, j, :, :].rearrange("p k e -> p (k e)"), ident)
                ins.then_inc(sm["f_gturned"], 1)

            def hidden(n, u, e, c):
                if e == 0 and c == 0:
                    pe.wait_ge(sm["f_xh"], n + 1)
                    pe.wait_ge(sm["f_xl"], n + 1)
                at = slice(c * P, (c + 1) * P)
                o = ps[:, C * (e % 2) + c, :]
                reached(pe, sm["f_relu"], (n * E + e - 2) * C + c + 1)
                nc.tensor.matmul(o, W1h[:, e, at], xh[:, u, :], start=True, stop=False)
                nc.tensor.matmul(o, W1h[:, e, at], xl[:, u, :], start=False, stop=False)
                nc.tensor.matmul(o, W1l[:, e, at], xh[:, u, :], start=False, stop=True).then_inc(sm["f_hidden"], 1)

            def biases(n, u):
                pe.wait_ge(sm["f_gateT"], n + 1)
                reached(pe, sm["f_output"], n)
                nc.tensor.matmul(ps[:, OUTPUT, :], b2p[:, :], gateT[:, u, :], start=True, stop=False)

            def expert(n, e):
                m, o = n * E + e, ps[:, OUTPUT, :]
                for c in range(C):
                    pe.wait_ge(sm["f_high"], m * C + c + 1)
                    nc.tensor.matmul(o, W2h[:, e, c, :], gh[:, e % 2, c, :], start=False, stop=False)
                    nc.tensor.matmul(o, W2l[:, e, c, :], gh[:, e % 2, c, :], start=False, stop=False)
                for c, low in enumerate(("f_low_dve", "f_low_pool")):
                    pe.wait_ge(sm[low], m + 1)
                    ins = nc.tensor.matmul(o, W2h[:, e, c, :], gl[:, e % 2, c, :], start=False,
                                           stop=(e == E - 1 and c == C - 1))
                ins.then_inc(sm["f_expert"], 1)

            def back(n):
                pe.wait_ge(sm["f_output"], n + 1)
                reached(pe, sm["f_added"], n)
                for j in range(J):
                    ins = nc.tensor.transpose(ps[:, BACK, j * P:(j + 1) * P], yT[:, j * P:(j + 1) * P], ident)
                ins.then_inc(sm["f_back"], 1)

            def body(i):
                for u in range(2):
                    n = i * 2 + u + p * S
                    first = isinstance(i, int) and i * 2 + u == 0
                    last = isinstance(i, int) and i * 2 + u == S - 1
                    later = not (isinstance(i, int) and i * 2 + u >= S - 2)
                    for e in range(E):
                        for c in range(C):
                            if e < E - 2:
                                hidden(n, u, e + 2, c)
                            elif not last:
                                hidden(n + 1, 1 - u, e + 2 - E, c)
                        if e == 0:
                            biases(n, u)
                        expert(n, e)
                        if e == 0 and not first:
                            back(n - 1)
                        if e == AHEAD and not last:
                            turn_gates(n + 1)
                        if e == 5 and later:
                            turn(n + 2, u)
                        if e == 6 and later:
                            logits(n + 2)

            turn(p * S, 0)
            logits(p * S)
            turn_gates(p * S)
            if p == 0:
                pe.wait_ge(sm["w1_low"], 1)
            for e in range(2):
                for c in range(C):
                    hidden(p * S, 0, e, c)
            turn(p * S + 1, 1)
            logits(p * S + 1)
            if p == 0:
                pe.wait_ge(sm["w2_low"], 1)
                pe.wait_ge(sm["b2_set"], 1)
            pairs_of_sequences(pe, body)
            back(p * S + S - 1)

        def first_half_of_w1(dve):
            dve.wait_ge(sm["w1_in"], 16)
            nc.vector.tensor_copy(W1h[:, :, :], W1[:, :, :]).then_inc(sm["w1_high"], 1)

        def second_half_of_w1(dve):
            dve.wait_ge(sm["w1_high"], 1)
            nc.vector.tensor_tensor(W1l[:, :, :], W1[:, :, :], W1h[:, :, :].bitcast(F32), ALU.subtract).then_inc(sm["w1_low"], 1)

        def first_half_of_w2(act):
            act.wait_ge(sm["w2_in"], 16)
            nc.scalar.activation(W2h[:, :, :, :], W2[:, :, :, :], ACT.Copy).then_inc(sm["w2_high"], 1)

        def second_half_of_w2(pool):
            pool.wait_ge(sm["w2_high"], 1)
            nc.gpsimd.tensor_tensor(W2l[:, :, :, :], W2[:, :, :, :], W2h[:, :, :, :].bitcast(F32), ALU.subtract).then_inc(sm["w2_low"], 1)

        def halve_b2(dve):
            rows = slice(0, PARTS * E)
            nc.vector.tensor_copy(b2_high[:, :], b2[:, :]).then_inc(sm["b2_high_set"], 1)
            dve.wait_ge(sm["b2_high_set"], 1)
            nc.vector.tensor_tensor(b2_low[:, :], b2[:, :], b2_high[:, :].bitcast(F32), ALU.subtract).then_inc(sm["b2_low_set"], 1)
            dve.wait_ge(sm["b2_low_set"], 1)
            nc.vector.tensor_scalar(b2_low[:, :], b2_low[:, :], K[rows, B2_LOW:B2_LOW + 1], None, ALU.mult).then_inc(sm["b2_scaled"], 1)
            dve.wait_ge(sm["b2_scaled"], 1)
            nc.vector.scalar_tensor_tensor(b2p[:, :], b2_high[:, :].bitcast(F32), K[rows, B2_HIGH:B2_HIGH + 1], b2_low[:, :],
                                           ALU.mult, ALU.add).then_inc(sm["b2_set"], 1)

        def ffn_vector(dve, p):
            def low_rows(n, u):
                dve.wait_ge(sm["f_xh"], n + 1)
                reached(dve, sm["f_hidden"], (n - 1) * E * C)
                nc.vector.tensor_tensor(xl[:, u, :], ps[:, PREP, :], xh[:, u, :].bitcast(F32), ALU.subtract).then_inc(sm["f_xl"], 1)

            def ranking(n):
                dve.wait_ge(sm["f_logits"], n + 1)
                nc.vector.tensor_tensor(lg[:, :, :], ps[:, TURN, 0:J * E].rearrange("p (j e) -> p j e", e=E),
                                        bg[:, :].unsqueeze(1).to_broadcast([P, J, E]), ALU.add).then_inc(sm["f_lg"], 1)
                dve.wait_ge(sm["f_lg"], n + 1)
                other = lg[:, :, :].unsqueeze(2).to_broadcast([P, J, E, E])
                own = lg[:, :, :].unsqueeze(3).to_broadcast([P, J, E, E])
                reached(dve, sm["f_ranks"], n)
                nc.vector.tensor_tensor(equal[:, :, :, :], other, own, ALU.is_equal).then_inc(sm["f_equal"], 1)
                nc.vector.tensor_tensor(before[:, :, :, :], other, own, ALU.is_gt).then_inc(sm["f_before"], 1)
                nc.vector.tensor_reduce(top[:, :], lg[:, :, :], AX.X, ALU.max).then_inc(sm["f_top"], 1)
                dve.wait_ge(sm["f_top"], n + 1)
                nc.vector.tensor_tensor(below[:, :, :], lg[:, :, :], top[:, :].unsqueeze(2).to_broadcast([P, J, E]),
                                        ALU.subtract).then_inc(sm["f_below"], 1)

            def gating(n):
                dve.wait_ge(sm["f_ranks"], n + 1)
                nc.vector.tensor_reduce(rank[:, :, :], ranks[:, :, :, :], AX.X, ALU.add).then_inc(sm["f_rank"], 1)
                dve.wait_ge(sm["f_rank"], n + 1)
                dve.wait_ge(sm["f_weight"], n + 1)
                nc.vector.scalar_tensor_tensor(picked[:, :, :], rank[:, :, :], TOPK - 0.5, weight[:, :, :],
                                               ALU.is_lt, ALU.mult).then_inc(sm["f_picked"], 1)
                dve.wait_ge(sm["f_picked"], n + 1)
                nc.vector.tensor_reduce(total[:, :], picked[:, :, :], AX.X, ALU.add).then_inc(sm["f_total"], 1)
                dve.wait_ge(sm["f_total"], n + 1)
                nc.vector.reciprocal(inv[:, :], total[:, :]).then_inc(sm["f_inv"], 1)
                dve.wait_ge(sm["f_inv"], n + 1)
                reached(dve, sm["f_gturned"], n)
                nc.vector.scalar_tensor_tensor(gate_parts[:, :, 0, :], picked[:, :, :], 0.5,
                                               inv[:, :].unsqueeze(2).to_broadcast([P, J, E]), ALU.mult, ALU.mult).then_inc(sm["f_gate"], 1)

            def halve_gates(n):
                dve.wait_ge(sm["f_gate"], n + 1)
                nc.vector.tensor_copy(gate_parts[:, :, 1:PARTS:2, :].bitcast(F32R),
                                      gate_parts[:, :, 0:1, :].to_broadcast([P, J, 2, E])).then_inc(sm["f_gate_high"], 1)
                dve.wait_ge(sm["f_gate_high"], n + 1)
                nc.vector.tensor_tensor(gate_parts[:, :, 2, :], gate_parts[:, :, 0, :], gate_parts[:, :, 1, :],
                                        ALU.subtract).then_inc(sm["f_parts"], 1)

            def gate_hidden(n, u, e):
                m = n * E + e
                if e == 0:
                    dve.wait_ge(sm["f_gates_ahead"], 16 * (n + 1))
                if e == AHEAD:
                    dve.wait_ge(sm["f_gates_rest"], 16 * (n + 1))
                dve.wait_ge(sm["f_relu"], m * C + C)
                reached(dve, sm["f_high"], (m - 1) * C)
                reached(dve, sm["f_low_pool"], m - 1)
                nc.vector.tensor_tensor(gated[:, e % 2, :, :], hid[:, e % 2, :, :],
                                        gates_on_all[u][:, e:e + 1, :].to_broadcast([P, C, T]), ALU.mult).then_inc(sm["f_gated"], 1)

            def low(n, e):
                m = n * E + e
                dve.wait_ge(sm["f_high"], m * C + 1)
                reached(dve, sm["f_expert"], m - 1)
                nc.vector.tensor_tensor(gl[:, e % 2, 0, :], gated[:, e % 2, 0, :], gh[:, e % 2, 0, :].bitcast(F32),
                                        ALU.subtract).then_inc(sm["f_low_dve"], 1)

            def add(s, n):
                dve.wait_ge(sm["f_back"], n + 1)
                nc.vector.tensor_tensor(tokens(s), tokens(s), ps[:, BACK, :], ALU.add).then_inc(sm["f_added"], 1)

            def rows(s, n, u):
                norm_rows(dve, "f_", s, n, u, lambda rows, u, j: (xnf[:, u, j, :], rows), [("f_turned", n - 1)])

            def body(i):
                for u in range(2):
                    s = i * 2 + u
                    n = s + p * S
                    first = isinstance(i, int) and s == 0
                    last = isinstance(i, int) and s == S - 1
                    later = not (isinstance(i, int) and s >= S - 2)
                    for e in range(E):
                        if e < E - 1:
                            gate_hidden(n, u, e + 1)
                        elif not last:
                            gate_hidden(n + 1, 1 - u, 0)
                        if e == 1 and not last:
                            gating(n + 1)
                        if e == 2 and not last:
                            halve_gates(n + 1)
                        if e == 3 and not first:
                            add(s - 1, n - 1)
                        if later:
                            if e == 0:
                                if p == 0 and first:
                                    dve.wait_ge(sm["x_rest"], 16)
                                norm_stats(dve, "f_", s + 2, n + 2, u)
                            if e == 2:
                                norm_sums(dve, "f_", n + 2, u)
                            if e == 4:
                                rows(s + 2, n + 2, u)
                            if e == 6:
                                low_rows(n + 2, u)
                            if e == 7:
                                ranking(n + 2)
                        if e < E - 1:
                            low(n, e + 1)
                        elif not last:
                            low(n + 1, 0)

            if p == 1:
                dve.wait_ge(sm["a_added"], S * G)
            norm_stats(dve, "f_", 0, p * S, 0)
            norm_sums(dve, "f_", p * S, 0)
            if p == 0:
                first_half_of_w1(dve)
            rows(0, p * S, 0)
            if p == 0:
                second_half_of_w1(dve)
            low_rows(p * S, 0)
            ranking(p * S)
            gating(p * S)
            halve_gates(p * S)
            if p == 0:
                halve_b2(dve)
            norm_stats(dve, "f_", 1, p * S + 1, 1)
            norm_sums(dve, "f_", p * S + 1, 1)
            rows(1, p * S + 1, 1)
            low_rows(p * S + 1, 1)
            ranking(p * S + 1)
            gate_hidden(p * S, 0, 0)
            low(p * S, 0)
            pairs_of_sequences(dve, body)
            add(S - 1, p * S + S - 1)

        def ffn_scalar(act, p):
            def rows(n, u):
                act.wait_ge(sm["f_turned"], n + 1)
                reached(act, sm["f_logits"], n)
                nc.scalar.activation(xnT[:, :], ps[:, PREP, :], ACT.Copy).then_inc(sm["f_xnT"], 1)
                reached(act, sm["f_hidden"], (n - 1) * E * C)
                nc.scalar.activation(xh[:, u, :], ps[:, PREP, :], ACT.Copy).then_inc(sm["f_xh"], 1)

            def weights(n):
                act.wait_ge(sm["f_below"], n + 1)
                reached(act, sm["f_picked"], n)
                nc.scalar.activation(weight[:, :, :], below[:, :, :], ACT.Exp).then_inc(sm["f_weight"], 1)

            def gates(n, u):
                act.wait_ge(sm["f_gturned"], n + 1)
                reached(act, sm["f_expert"], (n - 1) * E)
                nc.scalar.activation(gateT[:, u, :], ps[0:PARTS * E, TURN, :], ACT.Copy).then_inc(sm["f_gateT"], 1)
                reached(act, sm["f_gates_stored"], 16 * (n - 1))
                nc.scalar.activation(gate_rows[:, u, :], ps[0:E, TURN, :], ACT.Copy).then_inc(sm["f_gate_rows"], 1)

            def relu(n, e):
                m = n * E + e
                reached(act, sm["f_gated"], m - 1)
                for c in range(C):
                    act.wait_ge(sm["f_hidden"], m * C + c + 1)
                    nc.scalar.activation(hid[:, e % 2, c, :], ps[:, C * (e % 2) + c, :], ACT.Relu,
                                         bias=b1[:, e * C + c:e * C + c + 1]).then_inc(sm["f_relu"], 1)

            def high(n, e):
                m = n * E + e
                act.wait_ge(sm["f_gated"], m + 1)
                reached(act, sm["f_expert"], m - 1)
                for c in range(C):
                    nc.scalar.activation(gh[:, e % 2, c, :], gated[:, e % 2, c, :], ACT.Copy).then_inc(sm["f_high"], 1)

            def output(n):
                act.wait_ge(sm["f_expert"], n * E + E)
                reached(act, sm["f_back"], n)
                nc.scalar.activation(yT[:, :], ps[:, OUTPUT, :], ACT.Copy).then_inc(sm["f_output"], 1)

            def body(i):
                for u in range(2):
                    n = i * 2 + u + p * S
                    first = isinstance(i, int) and i * 2 + u == 0
                    last = isinstance(i, int) and i * 2 + u == S - 1
                    later = not (isinstance(i, int) and i * 2 + u >= S - 2)
                    for e in range(E):
                        if e == 0 and not first:
                            output(n - 1)
                        if e < E - 2:
                            relu(n, e + 2)
                        elif not last:
                            relu(n + 1, e + 2 - E)
                        if e < E - 1:
                            high(n, e + 1)
                        elif not last:
                            high(n + 1, 0)
                        if e == AHEAD and not last:
                            gates(n + 1, 1 - u)
                        if e == 5 and later:
                            rows(n + 2, u)
                        if e == 0 and not last:
                            weights(n + 1)

            rows(p * S, 0)
            if p == 0:
                first_half_of_w2(act)
            weights(p * S)
            gates(p * S, 0)
            relu(p * S, 0)
            relu(p * S, 1)
            rows(p * S + 1, 1)
            high(p * S, 0)
            pairs_of_sequences(act, body)
            output(p * S + S - 1)

        def ffn_gpsimd(pool, p):
            def low(n, e):
                m = n * E + e
                pool.wait_ge(sm["f_high"], m * C + C)
                reached(pool, sm["f_expert"], m - 1)
                nc.gpsimd.tensor_tensor(gl[:, e % 2, 1, :], gated[:, e % 2, 1, :], gh[:, e % 2, 1, :].bitcast(F32),
                                        ALU.subtract).then_inc(sm["f_low_pool"], 1)

            def ties(n):
                pool.wait_ge(sm["f_equal"], n + 1)
                tri = K[:, TRI:TRI + E * E].unsqueeze(1).to_broadcast([P, J, E * E])
                nc.gpsimd.tensor_tensor(tied[:, :, :, :].rearrange("p j e f -> p j (e f)"),
                                        equal[:, :, :, :].rearrange("p j e f -> p j (e f)"), tri, ALU.mult).then_inc(sm["f_tied"], 1)
                pool.wait_ge(sm["f_before"], n + 1)
                pool.wait_ge(sm["f_tied"], n + 1)
                reached(pool, sm["f_rank"], n)
                nc.gpsimd.tensor_tensor(ranks[:, :, :, :], before[:, :, :, :], tied[:, :, :, :], ALU.add).then_inc(sm["f_ranks"], 1)

            def body(i):
                for u in range(2):
                    n = i * 2 + u + p * S
                    last = isinstance(i, int) and i * 2 + u == S - 1
                    later = not (isinstance(i, int) and i * 2 + u >= S - 2)
                    for e in range(E):
                        if e < E - 1:
                            low(n, e + 1)
                        elif not last:
                            low(n + 1, 0)
                        if later and e == 2:
                            norm_pool(pool, "f_", n + 2, u)
                        if later and e == 7:
                            ties(n + 2)

            norm_pool(pool, "f_", p * S, 0)
            ties(p * S)
            if p == 0:
                second_half_of_w2(pool)
            norm_pool(pool, "f_", p * S + 1, 1)
            ties(p * S + 1)
            low(p * S, 0)
            pairs_of_sequences(pool, body)


        def attn_tensor(pe):
            def turn(g, s, u, hg):
                if hg == 0:
                    pe.wait_ge(sm["a_xn"], s + 1)
                reached(pe, sm["a_query"], g)
                for j in range(J):
                    rows = xna[:, u, j, hg * Q:(hg + 1) * Q, :, :].rearrange("p q r i -> p (q r i)")
                    ins = nc.tensor.transpose(ps[:, PREP, j * P:(j + 1) * P], rows, ident)
                ins.then_inc(sm["a_turned"], 1)

            def norms(g):
                pe.wait_ge(sm["a_square"], g + 1)
                nc.tensor.matmul(ps[:, PREP, :], block_bf[:, :], square[:, :], start=True, stop=True).then_inc(sm["a_norms"], 1)

            def scores(g, b, kk):
                j, half = kk // 2, kk % 2
                if kk == 0:
                    pe.wait_ge(sm["a_query"], g + 1)
                reached(pe, sm["a_probs"], g * STAGES + kk - 1)
                at = slice(half * 2 * W, (half + 1) * 2 * W)
                for odd, keyed in enumerate((key_even, key_odd)):
                    ins = nc.tensor.matmul(ps[:, 2 * (kk % 2) + odd, :], keyed[at, b, j * P:(j + 1) * P], query[at, b, :],
                                           start=True, stop=True)
                ins.then_inc(sm["a_scores"], 1)

            def mix(g, s, u, b, hg, kk):
                j, half = kk // 2, kk % 2
                if kk == 0:
                    pe.wait_ge(sm["a_value"], s + 1)
                    reached(pe, sm["a_copied"], g - 1)
                pe.wait_ge(sm["a_probs"], g * STAGES + kk + 1)
                for odd in range(2):
                    q = 2 * half + odd
                    ins = nc.tensor.matmul(ps[q * W:(q + 1) * W, 4 + b, :], value[:, u, j, hg * Q + q, :],
                                           probs[:, kk % RING, odd, :], start=(j == 0), stop=(j == J - 1))
                ins.then_inc(sm["a_mixed"], 1)

            def back(g, b):
                pe.wait_ge(sm["a_copied"], g + 1)
                reached(pe, sm["a_normed"], g)
                for j in range(J):
                    ins = nc.tensor.transpose(ps[:, TURN, j * P:(j + 1) * P], mixed[:, b, j * P:(j + 1) * P], ident)
                ins.then_inc(sm["a_back"], 1)

            def body(i):
                for t in range(2 * G):
                    g, u, hg, b = i * 2 * G + t, t // G, t % G, t % 2
                    first = isinstance(i, int) and i * 2 * G + t == 0
                    last = isinstance(i, int) and i * 2 * G + t == S * G - 1
                    for kk in range(STAGES):
                        if kk < STAGES - 2:
                            scores(g, b, kk + 2)
                        elif not last:
                            scores(g + 1, 1 - b, kk + 2 - STAGES)
                        mix(g, i * 2 + u, u, b, hg, kk)
                        if kk == 3 and not last:
                            norms(g + 1)
                        if kk == 5 and not first:
                            back(g - 1, 1 - b)
                        if kk == 7 and not last and not (isinstance(i, int) and i * 2 * G + t == S * G - 2):
                            turn(g + 2, i * 2 + (t + 2) // G, (t + 2) // G % 2, (t + 2) % G)

            pe.wait_ge(sm["f_relu"], S * E * C)
            pe.wait_ge(sm["f_gated"], S * E)
            pe.wait_ge(sm["f_output"], S)
            pe.wait_ge(sm["f_added"], S)
            turn(0, 0, 0, 0)
            norms(0)
            turn(1, 0, 0, 1)
            scores(0, 0, 0)
            scores(0, 0, 1)
            pairs_of_sequences(pe, body)
            back(S * G - 1, 1)

        def attn_vector(dve):
            def centre(g):
                dve.wait_ge(sm["a_turned"], g + 1)
                nc.vector.reduce_sum(negsum[:, :], ps[:, PREP, :], AX.X, negate=True).then_inc(sm["a_sum"], 1)
                dve.wait_ge(sm["a_sum"], g + 1)
                reached(dve, sm["a_square"], g)
                nc.vector.tensor_scalar(cent[:, :], ps[:, PREP, :], CENTRED, negsum[:, :], ALU.mult, ALU.add).then_inc(sm["a_cent"], 1)

            def operands(g, b):
                dve.wait_ge(sm["a_cent"], g + 1)
                nc.vector.tensor_copy(high[:, :], cent[:, :]).then_inc(sm["a_high"], 1)
                dve.wait_ge(sm["a_high"], g + 1)
                nc.vector.scalar_tensor_tensor(keys[:, :], high[:, :], const(KEY_LO), cent[:, :],
                                               ALU.mult, ALU.add).then_inc(sm["a_keys"], 1)
                nc.vector.scalar_tensor_tensor(part[:, :], high[:, :], const(QUERY_LO), cent[:, :],
                                               ALU.mult, ALU.add).then_inc(sm["a_part"], 1)
                dve.wait_ge(sm["a_keys"], g + 1)
                reached(dve, sm["a_scores"], (g - 1) * STAGES)
                nc.vector.tensor_scalar(key_even[:, b, :], keys[:, :], const(KEEP_EVEN), const(UNIT_EVEN), ALU.mult, ALU.add)
                nc.vector.tensor_scalar(key_odd[:, b, :], keys[:, :], const(KEEP_ODD), const(UNIT_ODD), ALU.mult, ALU.add).then_inc(sm["a_keyed"], 1)
                dve.wait_ge(sm["a_part"], g + 1)
                dve.wait_ge(sm["a_norms"], g + 1)
                nc.vector.scalar_tensor_tensor(query[:, b, :], ps[:, PREP, :], const(SHIFT_ROW), part[:, :],
                                               ALU.mult, ALU.add).then_inc(sm["a_query"], 1)

            def copy(g, b):
                dve.wait_ge(sm["a_mixed"], g * STAGES + STAGES)
                reached(dve, sm["a_back"], g - 1)
                nc.vector.tensor_copy(mixed[:, b, :], ps[:, 4 + b, :]).then_inc(sm["a_copied"], 1)

            def finish(g, s, hg):
                dve.wait_ge(sm["a_back"], g + 1)
                back = ps[:, TURN, :].rearrange("p (j q w) -> p j q w", j=J, q=Q)
                nc.vector.reciprocal(recip[:, :, :], back[:, :, :, HD]).then_inc(sm["a_recip"], 1)
                dve.wait_ge(sm["a_recip"], g + 1)
                nc.vector.tensor_tensor(normed[:, :, :, :], back[:, :, :, 0:HD],
                                        recip[:, :, :].unsqueeze(3).to_broadcast([P, J, Q, HD]), ALU.mult).then_inc(sm["a_normed"], 1)
                dve.wait_ge(sm["a_normed"], g + 1)
                rows = tokens(s).rearrange("p (j d) -> p j d", j=J)[:, :, hg * Q * HD:(hg + 1) * Q * HD]
                nc.vector.tensor_tensor(rows, rows, normed[:, :, :, :].rearrange("p j q i -> p j (q i)"),
                                        ALU.add).then_inc(sm["a_added"], 1)

            def rows(s, u):
                def copies(rows, u, j):
                    rows = rows.rearrange("p (h i) -> p h i", i=HD).unsqueeze(2).to_broadcast([P, H, REP, HD])
                    return xna[:, u, j, :, :, :], rows
                norm_rows(dve, "a_", s, s, u, copies, [("a_turned", (s - 1) * G), ("a_value", s - 1)])

            def body(i):
                for t in range(2 * G):
                    g, s, u, hg, b = i * 2 * G + t, i * 2 + t // G, t // G, t % G, t % 2
                    first = isinstance(i, int) and i * 2 * G + t == 0
                    last = isinstance(i, int) and i * 2 * G + t == S * G - 1
                    if not last:
                        centre(g + 1)
                    if not first:
                        copy(g - 1, 1 - b)
                    if not last:
                        operands(g + 1, 1 - b)
                    if not first:
                        finish(g - 1, i * 2 + (t - 1) // G, (t - 1) % G)
                    if not (isinstance(i, int) and s == S - 1):
                        if hg == 0:
                            norm_stats(dve, "a_", s + 1, s + 1, 1 - u)
                            norm_sums(dve, "a_", s + 1, 1 - u)
                        if hg == 1:
                            rows(s + 1, 1 - u)

            dve.wait_ge(sm["f_added"], S)
            norm_stats(dve, "a_", 0, 0, 0)
            norm_sums(dve, "a_", 0, 0)
            rows(0, 0)
            centre(0)
            operands(0, 0)
            pairs_of_sequences(dve, body)
            copy(S * G - 1, 1)
            finish(S * G - 1, S - 1, G - 1)

        def attn_scalar(act):
            def body(i):
                for t in range(2 * G):
                    g = i * 2 * G + t
                    for kk in range(STAGES):
                        act.wait_ge(sm["a_scores"], g * STAGES + kk + 1)
                        reached(act, sm["a_mixed"], g * STAGES + kk - RING + 1)
                        nc.scalar.activation(probs[:, kk % RING, :, :], ps[:, 2 * (kk % 2):2 * (kk % 2) + 2, :], ACT.Exp,
                                             bias=const(MINUS_SHIFT), scale=SCORE).then_inc(sm["a_probs"], 1)
            pairs_of_sequences(act, body)

        def attn_gpsimd(pool):
            def square_rows(g):
                pool.wait_ge(sm["a_cent"], g + 1)
                reached(pool, sm["a_norms"], g)
                nc.gpsimd.tensor_tensor(square[:, :], cent[:, :], cent[:, :], ALU.mult).then_inc(sm["a_square"], 1)

            def values_due(s):
                pool.wait_ge(sm["a_xn"], s + 1)
                reached(pool, sm["a_mixed"], (s - 1) * G * STAGES)

            def values(u):
                for j in range(J):
                    ins = nc.gpsimd.tensor_copy(value[:, u, j, :, 0:HD], xna[:, u, j, :, 0, :])
                ins.then_inc(sm["a_value"], 1)

            def body(i):
                for t in range(2 * G):
                    g, s, u, hg = i * 2 * G + t, i * 2 + t // G, t // G, t % G
                    more = not (isinstance(i, int) and s == S - 1)
                    if hg == 2 and more:
                        values_due(s + 1)
                    if not (isinstance(i, int) and i * 2 * G + t == S * G - 1):
                        square_rows(g + 1)
                    if hg == 0 and more:
                        norm_pool(pool, "a_", s + 1, 1 - u)
                    if hg == 2 and more:
                        values(1 - u)

            norm_pool(pool, "a_", 0, 0)
            values_due(0)
            square_rows(0)
            values(0)
            pairs_of_sequences(pool, body)

        @block.gpsimd
        def _(pool):
            nc.gpsimd.memset(value[:, :, :, :, :], 0.0).then_inc(sm["value_set"], 1)
            pool.wait_ge(sm["value_set"], 1)
            nc.gpsimd.memset(value[:, :, :, :, HD:HD + 1], 1.0).then_inc(sm["value_set"], 1)
            pool.wait_ge(sm["value_set"], 2)
            pool.wait_ge(sm["const_in"], 16)
            ffn_gpsimd(pool, 0)
            attn_gpsimd(pool)
            ffn_gpsimd(pool, 1)

        @block.tensor
        def _(pe):
            pe.wait_ge(sm["const_in"], 16)
            pe.wait_ge(sm["small_in"], 16 * 7)
            nc.tensor.transpose(ps[:, TURN, 0:E * C], b1r[:, :], ident[0:E * C, 0:E * C]).then_inc(sm["b1_turned"], 1)
            pe.wait_ge(sm["b1_set"], 1)
            pe.wait_ge(sm["block_set"], 1)
            ffn_tensor(pe, 0)
            attn_tensor(pe)
            pe.wait_ge(sm["a_probs"], S * G * STAGES)
            pe.wait_ge(sm["a_added"], S * G)
            ffn_tensor(pe, 1)

        @block.scalar
        def _(act):
            act.dma_start(K[:, :], const_in).then_inc(sm["const_in"], 16)
            act.dma_start(W1[:, :, :], w1_in.rearrange("e d f -> d e f")).then_inc(sm["w1_in"], 16)
            act.dma_start(W2[:, :, :, :], w2_in.rearrange("e (c p) d -> p e c d", c=C)).then_inc(sm["w2_in"], 16)
            act.wait_ge(sm["b1_turned"], 1)
            nc.scalar.activation(b1[:, :], ps[:, TURN, 0:E * C], ACT.Copy).then_inc(sm["b1_set"], 1)
            act.wait_ge(sm["b1_set"], 1)
            ffn_scalar(act, 0)
            attn_scalar(act)
            ffn_scalar(act, 1)

        @block.vector
        def _(dve):
            dve.wait_ge(sm["const_in"], 16)
            nc.vector.tensor_copy(block_bf[:, :], K[:, BLOCK:BLOCK + P]).then_inc(sm["block_set"], 1)
            dve.wait_ge(sm["small_in"], 16 * 7)
            dve.wait_ge(sm["x_first"], 16)
            ffn_vector(dve, 0)
            attn_vector(dve)
            ffn_vector(dve, 1)


def kernel(**inputs):
    import concourse.bacc as bacc
    from concourse.bass_utils import run_bass_kernel_spmd as run

    nc = bacc.Bacc("TRN2", target_bir_lowering=False, num_devices=1)
    names = ["L0_attn_x", "L0_ffn_Wg", "L0_ffn_bg", "L0_ffn_W1", "L0_ffn_b1", "L0_ffn_W2", "L0_ffn_b2"]
    arrays = {"in_" + n: np.ascontiguousarray(inputs[n]) for n in names}
    arrays["in_constants"] = constants()
    args = [nc.dram_tensor(n, a.shape, F32, kind="ExternalInput").ap() for n, a in arrays.items()]
    out = nc.dram_tensor("out", (S, T, D), F32, kind="ExternalOutput").ap()
    gates_dram = nc.dram_tensor("gates", (2, E, T), F32, kind="Internal").ap()
    build(nc, *args, gates_dram, out)
    return run(nc, [arrays], core_ids=[0]).results[0]["out"]
```

```python
from contextlib import ExitStack

import concourse.bass as bass
import numpy as np
from concourse import mybir

P = 128
S, T, D = 16, 512, 128
J = T // P
E, F = 8, 256
C = F // P
TOPK = 2
PARTS = 4
AHEAD = 2
H, HD = 16, 8
Q = 4
G = H // Q
W = P // Q
STAGES = J * 2
REP = W // HD
EPS = 1e-5
CENTRED = float(T)
SCORE = 1.0 / CENTRED ** 2
UNIT_ROWS = 4096.0
SHIFT = 50.0

F32, F16, BF16 = mybir.dt.float32, mybir.dt.float16, mybir.dt.bfloat16
F32R = mybir.dt.float32r
ALU = mybir.AluOpType
ACT = mybir.ActivationFunctionType
AX = mybir.AxisListType

IDENT, BLOCK, TRI = 0, P, 2 * P
KEY_LO, QUERY_LO, SHIFT_ROW, KEEP_EVEN, UNIT_EVEN, KEEP_ODD, UNIT_ODD, MINUS_HALF, MINUS_SHIFT, B2_HIGH, B2_LOW, HALF, APART, PER_COLUMN, EPSILON = range(
    TRI + E * E, TRI + E * E + 15)
NCONST = TRI + E * E + 15


def constants():
    c = np.zeros((P, NCONST), np.float32)
    row = np.arange(P)
    quadrant, copy = row // W, row % W // HD
    c[:, IDENT:IDENT + P] = np.eye(P)
    c[:, BLOCK:BLOCK + P] = (quadrant[:, None] == quadrant[None, :]) & (copy == 0)[:, None]
    c[:, TRI:TRI + E * E] = (np.arange(E)[None, :] < np.arange(E)[:, None]).reshape(-1)
    c[:, KEY_LO] = -1.0 * (copy == 1)
    c[:, QUERY_LO] = -1.0 * (copy >= 2)
    c[:, SHIFT_ROW] = -1.0 / (UNIT_ROWS * HD) * (copy == 3)
    for odd, keep, unit in ((0, KEEP_EVEN, UNIT_EVEN), (1, KEEP_ODD, UNIT_ODD)):
        c[:, keep] = (quadrant % 2 == odd) & (copy < 3)
        c[:, unit] = UNIT_ROWS * ((quadrant % 2 == odd) & (copy == 3))
    c[:, MINUS_HALF] = -0.5
    c[:, MINUS_SHIFT] = -SHIFT
    c[:, HALF], c[:, APART], c[:, PER_COLUMN], c[:, EPSILON] = 0.5, D / 4.0, 1.0 / D, EPS
    c[:, B2_HIGH] = (E <= row) & (row < 3 * E)
    c[:, B2_LOW] = (3 * E <= row) & (row < 4 * E)
    return c


def reached(eng, sem, value):
    if not isinstance(value, int) or value > 0:
        eng.wait_ge(sem, value)


def groups_after(g):
    return S * G - 1 - g if isinstance(g, int) else S * G


def pairs_of_sequences(eng, body):
    n = S // 2
    body(0)
    with eng.Fori(1, n - 1) as i:
        body(i)
    body(n - 1)


def build(nc, x_in, wg_in, bg_in, w1_in, b1_in, w2_in, b2_in, const_in, gates_dram, out):
    with ExitStack() as ctx:
        def sb(name, shape, dt=F32):
            return ctx.enter_context(nc.sbuf_tensor(name, shape, dt))

        def sem(name):
            return ctx.enter_context(nc.semaphore(name))

        X = sb("X", [P, S * J * D])
        W1 = sb("W1", [P, E, F])
        W1h, W1l = sb("W1h", [P, E, F], F32R), sb("W1l", [P, E, F], F32R)
        W2h, W2l = sb("W2h", [P, E, C, D], F32R), sb("W2l", [P, E, C, D], F32R)
        WG = sb("WG", [P, W])
        bg = sb("bg", [P, E])
        b1r = sb("b1r", [E * C, P])
        b1 = sb("b1", [P, E * C])
        b2 = sb("b2", [PARTS * E, D])
        b2_high = sb("b2_high", [PARTS * E, D], F32R)
        b2_low = sb("b2_low", [PARTS * E, D])
        b2p = sb("b2p", [PARTS * E, D], F32R)
        K = sb("K", [P, NCONST])
        block_bf = sb("block_bf", [P, P], BF16)
        ident = K[:, IDENT:IDENT + P]

        def const(n):
            return K[:, n:n + 1]

        stats = sb("stats", [P, 2, J, 6])
        halves = sb("halves", [P, J, 2])
        apart = sb("apart", [P, J])
        spread = sb("spread", [P, J])
        squares = sb("squares", [P, J])
        mean = sb("mean", [P, 2, J])
        between = sb("between", [P, J])
        var = sb("var", [P, J])
        vare = sb("vare", [P, J])
        rstd = sb("rstd", [P, 2, J])
        xnf = sb("xnf", [P, 2, J, D])
        xnT = sb("xnT", [P, T])
        xh, xl = sb("xh", [P, 2, T], F32R), sb("xl", [P, 2, T], F32R)
        logit_rows = sb("logit_rows", [P, P])
        lg = sb("lg", [P, J, E])
        before = sb("before", [P, J, E, E])
        equal = sb("equal", [P, J, E, E])
        tied = sb("tied", [P, J, E, E])
        ranks = sb("ranks", [P, J, E, E])
        rank = sb("rank", [P, J, E])
        top = sb("top", [P, J])
        below = sb("below", [P, J, E])
        weight = sb("weight", [P, J, E])
        picked = sb("picked", [P, J, E])
        total = sb("total", [P, J])
        inv = sb("inv", [P, J])
        gate_parts = sb("gate_parts", [P, J, PARTS, E])
        gateT = sb("gateT", [PARTS * E, 2, T], F32R)
        gate_rows = sb("gate_rows", [E, 2, T])
        hid = sb("hid", [P, 2, C, T])
        gated = sb("gated", [P, 2, C, T])
        gh, gl = sb("gh", [P, 2, C, T], F32R), sb("gl", [P, 2, C, T], F32R)
        yT = sb("yT", [P, T])
        xna = sb("xna", [P, 2, J, H, REP, HD])
        value = sb("value", [P, 2, J, H, W])
        negsum = sb("negsum", [P, 1])
        cent = sb("cent", [P, T])
        high = sb("high", [P, T], F16)
        square = sb("square", [P, T], BF16)
        keys = sb("keys", [P, T], F16)
        part = sb("part", [P, T], F16)
        key_even = sb("key_even", [P, 2, T], F16)
        key_odd = sb("key_odd", [P, 2, T], F16)
        query = sb("query", [P, 2, T], F16)
        probs = sb("probs", [P, STAGES // 2, 2, T])
        ring = [probs[:, k, :, :] for k in range(STAGES // 2)] + [rows[:, k, :, :] for rows in (hid, gated) for k in range(2)]
        mixed = sb("mixed", [P, 2, T])
        gates_on_all = [probs[:, :, :, :].rearrange("p r o t -> p (r o t)").rearrange("p (e t) -> p e t", e=E),
                        xna[:, :, :, :, :, :].rearrange("p u j h r i -> p (u j h r i)").rearrange("p (e t) -> p e t", e=E)]
        W2 = xna[:, 0, :, :, :, :].rearrange("p j h r i -> p (j h r i)").rearrange("p (e c d) -> p e c d", e=E, c=C)
        recip = sb("recip", [P, J, Q])
        normed = sb("normed", [P, J, Q, HD])

        ps = ctx.enter_context(nc.psum_tensor("ps", [P, 8, T], F32))
        OUTPUT = (4, 5)
        PREP, TURN = 6, 7

        names = """const_in w1_in w2_in small_in x_first x_rest stored value_set block_set wg_cleared b1_turned b1_set
            w1_high w1_low w2_high w2_low b2_high_set b2_low_set b2_scaled b2_set
            f_halves f_apart f_mean f_spread f_between f_squares f_var f_vare f_rstd f_xn f_turned f_xnT f_xh f_xl f_logits f_logit_rows f_logits_turned f_lg f_before
            f_equal f_tied f_ranks f_rank f_top f_below f_weight f_picked f_total f_inv f_gate f_gate_high
            f_parts f_gturned f_gateT f_gate_rows f_gates_stored f_gates_ahead f_gates_rest
            f_stats f_hidden f_relu f_gated f_high f_low_dve f_low_pool f_expert
            f_output f_back f_added
            a_stats a_halves a_apart a_mean a_spread a_between a_squares a_var a_vare a_rstd a_xn a_value a_turned a_sum a_cent a_high a_square a_norms a_keys a_part
            a_keyed a_query a_scores a_probs a_mixed a_copied a_back a_recip a_normed a_added""".split()
        sm = {n: sem(n) for n in names}

        block = ctx.enter_context(nc.Block())

        xs_in = x_in.rearrange("s (p j) d -> p s (j d)", j=J)
        xs_out = out.rearrange("s (p j) d -> p s (j d)", j=J)

        def tokens(s, j=0, n=J):
            return X[:, bass.ds((s * J + j) * D, n * D)]

        @block.sync
        def _(sp):
            sp.dma_start(X[:, 0:2 * J * D].rearrange("p (s c) -> p s c", s=2), xs_in[:, 0:2]).then_inc(sm["x_first"], 16)
            sp.wait_ge(sm["wg_cleared"], 1)
            sp.dma_start(WG[:, 0:E], wg_in).then_inc(sm["small_in"], 16)
            sp.dma_start(bg[:, :], bg_in.rearrange("(a e) -> a e", a=1).to_broadcast([P, E])).then_inc(sm["small_in"], 16)
            sp.dma_start(b1r[:, :], b1_in.rearrange("e (c p) -> (e c) p", c=C)).then_inc(sm["small_in"], 16)
            for k in range(PARTS):
                sp.dma_start(b2[k * E:(k + 1) * E, :], b2_in).then_inc(sm["small_in"], 16)
            sp.dma_start(X[:, 2 * J * D:].rearrange("p (s c) -> p s c", c=J * D), xs_in[:, 2:]).then_inc(sm["x_rest"], 16)

            def spread_gates(n, u):
                sp.wait_ge(sm["f_gate_rows"], n + 1)
                sp.dma_start(gates_dram[u], gate_rows[:, u, :]).then_inc(sm["f_gates_stored"], 16)
                sp.wait_ge(sm["f_gates_stored"], 16 * (n + 1))
                for done, experts in (("f_gates_ahead", slice(0, AHEAD)), ("f_gates_rest", slice(AHEAD, E))):
                    sp.dma_start(gates_on_all[u][:, experts, :], gates_dram[u:u + 1, experts, :].to_broadcast(
                        [P, experts.stop - experts.start, T])).then_inc(sm[done], 16)

            def store(s):
                sp.wait_ge(sm["f_added"], S + s + 1)
                sp.dma_start(xs_out[:, bass.ds(s, 1)],
                             tokens(s).rearrange("p (s c) -> p s c", s=1)).then_inc(sm["stored"], 16)

            for p in range(2):
                def body(i):
                    for u in range(2):
                        s = i * 2 + u
                        if p == 1 and not (isinstance(i, int) and s == 0):
                            store(s - 1)
                        if not (isinstance(i, int) and s == S - 1):
                            if p == 0 and isinstance(i, int) and s == 0:
                                sp.wait_ge(sm["w2_low"], 1)
                            spread_gates(p * S + s + 1, 1 - u)

                if p == 1:
                    sp.wait_ge(sm["a_mixed"], S * G * STAGES)
                    sp.wait_ge(sm["a_turned"], S * G)
                    sp.wait_ge(sm["a_value"], S)
                spread_gates(p * S, 0)
                pairs_of_sequences(sp, body)
            store(S - 1)
            sp.wait_ge(sm["stored"], 16 * S)

        def norm_stats(dve, a, s, n, u):
            for j in range(J):
                nc.vector.bn_stats(stats[:, u, j, :], tokens(s, j, 1)).then_inc(sm[a + "stats"], 1)

        def norm_rows(dve, a, s, n, u, into, free):
            dve.wait_ge(sm[a + "mean"], n + 1)
            dve.wait_ge(sm[a + "rstd"], n + 1)
            for sem_name, count in free:
                reached(dve, sm[sem_name], count)
            for j in range(J):
                to, rows = into(tokens(s, j, 1), u, j)
                ins = nc.vector.tensor_scalar(to, rows, mean[:, u, j:j + 1], rstd[:, u, j:j + 1],
                                              ALU.subtract, ALU.mult)
            ins.then_inc(sm[a + "xn"], 1)

        def each(column):
            return const(column).to_broadcast([P, J])

        def norm_means(pool, a, n, u):
            even, odd = stats[:, u, :, 1:3], stats[:, u, :, 4:6]
            pool.wait_ge(sm[a + "stats"], n * J + J)
            nc.gpsimd.tensor_tensor(apart[:, :], even[:, :, 0], odd[:, :, 0], ALU.subtract).then_inc(sm[a + "apart"], 1)
            nc.gpsimd.tensor_tensor(halves[:, :, :], even, odd, ALU.add).then_inc(sm[a + "halves"], 1)
            pool.wait_ge(sm[a + "apart"], n + 1)
            nc.gpsimd.tensor_tensor(spread[:, :], apart[:, :], apart[:, :], ALU.mult).then_inc(sm[a + "spread"], 1)
            pool.wait_ge(sm[a + "halves"], n + 1)
            nc.gpsimd.tensor_tensor(mean[:, u, :], halves[:, :, 0], each(HALF), ALU.mult).then_inc(sm[a + "mean"], 1)
            pool.wait_ge(sm[a + "spread"], n + 1)
            nc.gpsimd.tensor_tensor(between[:, :], spread[:, :], each(APART), ALU.mult).then_inc(sm[a + "between"], 1)

        def norm_variances(pool, a, n):
            pool.wait_ge(sm[a + "between"], n + 1)
            nc.gpsimd.tensor_tensor(squares[:, :], between[:, :], halves[:, :, 1], ALU.add).then_inc(sm[a + "squares"], 1)
            pool.wait_ge(sm[a + "squares"], n + 1)
            nc.gpsimd.tensor_tensor(var[:, :], squares[:, :], each(PER_COLUMN), ALU.mult).then_inc(sm[a + "var"], 1)
            pool.wait_ge(sm[a + "var"], n + 1)
            nc.gpsimd.tensor_tensor(vare[:, :], var[:, :], each(EPSILON), ALU.add).then_inc(sm[a + "vare"], 1)

        def norm_powers(pool, a, n, u):
            pool.wait_ge(sm[a + "vare"], n + 1)
            nc.gpsimd.tensor_tensor(rstd[:, u, :], vare[:, :], each(MINUS_HALF), ALU.pow).then_inc(sm[a + "rstd"], 1)

        def norm_pool(pool, a, n, u):
            norm_means(pool, a, n, u)
            norm_variances(pool, a, n)
            norm_powers(pool, a, n, u)

        def routing_bank(n):
            return OUTPUT[0] if isinstance(n, int) and n % S == 0 else TURN

        def ffn_turn(pe, n, u):
            pe.wait_ge(sm["f_xn"], n + 1)
            reached(pe, sm["f_xl"], n)
            if isinstance(n, int) and n == S:
                pe.wait_ge(sm["a_query"], S * G)
            for j in range(J):
                ins = nc.tensor.transpose(ps[:, PREP, j * P:(j + 1) * P], xnf[:, u, j, :], ident)
            ins.then_inc(sm["f_turned"], 1)

        def ffn_logits(pe, n):
            pe.wait_ge(sm["f_xnT"], n + 1)
            reached(pe, sm["f_gate_rows"], n)
            if isinstance(n, int) and n == S:
                pe.wait_ge(sm["a_copied"], S * G - 1)
            if isinstance(n, int) and n == S + 1:
                pe.wait_ge(sm["a_normed"], S * G)
            for j in range(J):
                ins = nc.tensor.matmul(ps[j * W:(j + 1) * W, routing_bank(n), 0:P], WG[:, :], xnT[:, j * P:(j + 1) * P],
                                       start=True, stop=True)
            ins.then_inc(sm["f_logits"], 1)

        def ffn_turn_logits(pe, n):
            pe.wait_ge(sm["f_logit_rows"], n + 1)
            nc.tensor.transpose(ps[:, routing_bank(n), P:2 * P], logit_rows[:, :], ident).then_inc(sm["f_logits_turned"], 1)

        def ffn_turn_gates(pe, n):
            pe.wait_ge(sm["f_parts"], n + 1)
            for j in range(J):
                ins = nc.tensor.transpose(ps[0:PARTS * E, routing_bank(n), j * P:(j + 1) * P],
                                          gate_parts[:, j, :, :].rearrange("p k e -> p (k e)"), ident)
            ins.then_inc(sm["f_gturned"], 1)

        def ffn_back(pe, n, u):
            pe.wait_ge(sm["f_output"], n + 1)
            for j in range(J):
                ins = nc.tensor.transpose(ps[:, OUTPUT[u], j * P:(j + 1) * P], yT[:, j * P:(j + 1) * P], ident)
            ins.then_inc(sm["f_back"], 1)

        def ffn_tensor(pe, p):
            def hidden(n, u, e, c):
                if e == 0 and c == 0:
                    pe.wait_ge(sm["f_xh"], n + 1)
                    pe.wait_ge(sm["f_xl"], n + 1)
                at = slice(c * P, (c + 1) * P)
                o = ps[:, C * (e % 2) + c, :]
                reached(pe, sm["f_relu"], (n * E + e - 2) * C + c + 1)
                nc.tensor.matmul(o, W1h[:, e, at], xh[:, u, :], start=True, stop=False)
                nc.tensor.matmul(o, W1h[:, e, at], xl[:, u, :], start=False, stop=False)
                nc.tensor.matmul(o, W1l[:, e, at], xh[:, u, :], start=False, stop=True).then_inc(sm["f_hidden"], 1)

            def biases(n, u):
                pe.wait_ge(sm["f_gateT"], n + 1)
                if isinstance(n, int) and n % S == 0:
                    pe.wait_ge(sm["f_gate_rows"], n + 1)
                reached(pe, sm["f_added"], n - 1)
                nc.tensor.matmul(ps[:, OUTPUT[u], :], b2p[:, :], gateT[:, u, :], start=True, stop=False)

            def expert(n, u, e):
                m, o = n * E + e, ps[:, OUTPUT[u], :]
                for c in range(C):
                    pe.wait_ge(sm["f_high"], m * C + c + 1)
                    nc.tensor.matmul(o, W2h[:, e, c, :], gh[:, e % 2, c, :], start=False, stop=False)
                    nc.tensor.matmul(o, W2l[:, e, c, :], gh[:, e % 2, c, :], start=False, stop=False)
                for c, low in ((1, "f_low_dve"), (0, "f_low_pool")):
                    pe.wait_ge(sm[low], m + 1)
                    ins = nc.tensor.matmul(o, W2h[:, e, c, :], gl[:, e % 2, c, :], start=False,
                                           stop=(e == E - 1 and c == 0))
                ins.then_inc(sm["f_expert"], 1)

            def body(i):
                for u in range(2):
                    n = i * 2 + u + p * S
                    first = isinstance(i, int) and i * 2 + u == 0
                    last = isinstance(i, int) and i * 2 + u == S - 1
                    later = not (isinstance(i, int) and i * 2 + u >= S - 2)
                    for e in range(E):
                        for c in range(C):
                            if e < E - 2:
                                hidden(n, u, e + 2, c)
                            elif not last:
                                hidden(n + 1, 1 - u, e + 2 - E, c)
                        if e == 0:
                            biases(n, u)
                        expert(n, u, e)
                        if e == 0 and not first:
                            ffn_back(pe, n - 1, 1 - u)
                        if e == AHEAD + 1 and not last:
                            ffn_turn_gates(pe, n + 1)
                        if e == 4 and later:
                            ffn_turn(pe, n + 2, u)
                        if e == 5 and later:
                            ffn_logits(pe, n + 2)
                        if e == 6 and later:
                            ffn_turn_logits(pe, n + 2)
                        if p == 0 and last:
                            if e == 4:
                                attn_turn(pe, 0, 0, 0, 0)
                            if e == 6:
                                attn_norms(pe, 0)
                            if e == 7:
                                attn_turn(pe, 1, 0, 0, 1)

            if p == 0:
                ffn_turn(pe, 0, 0)
                pe.wait_ge(sm["small_in"], 16 * 7)
                nc.tensor.transpose(ps[:, TURN, 0:E * C], b1r[:, :], ident[0:E * C, 0:E * C]).then_inc(sm["b1_turned"], 1)
                ffn_logits(pe, 0)
                ffn_turn_logits(pe, 0)
            if p == 0:
                pe.wait_ge(sm["w1_low"], 1)
            for e in range(2):
                for c in range(C):
                    hidden(p * S, 0, e, c)
                if p == 0 and e == 0:
                    ffn_turn_gates(pe, 0)
            if p == 0:
                pe.wait_ge(sm["b1_set"], 1)
            ffn_turn(pe, p * S + 1, 1)
            ffn_logits(pe, p * S + 1)
            ffn_turn_logits(pe, p * S + 1)
            if p == 0:
                pe.wait_ge(sm["w2_low"], 1)
                pe.wait_ge(sm["b2_set"], 1)
            pairs_of_sequences(pe, body)

        def first_half_of_w1(dve):
            dve.wait_ge(sm["w1_in"], 16)
            nc.vector.tensor_copy(W1h[:, :, :], W1[:, :, :]).then_inc(sm["w1_high"], 1)

        def second_half_of_w1(dve):
            dve.wait_ge(sm["w1_high"], 1)
            nc.vector.tensor_tensor(W1l[:, :, :], W1[:, :, :], W1h[:, :, :].bitcast(F32), ALU.subtract).then_inc(sm["w1_low"], 1)

        def first_half_of_w2(act):
            act.wait_ge(sm["w2_in"], 16)
            nc.scalar.activation(W2h[:, :, :, :], W2[:, :, :, :], ACT.Copy).then_inc(sm["w2_high"], 1)

        def second_half_of_w2(pool):
            pool.wait_ge(sm["w2_high"], 1)
            nc.gpsimd.tensor_tensor(W2l[:, :, :, :], W2[:, :, :, :], W2h[:, :, :, :].bitcast(F32), ALU.subtract).then_inc(sm["w2_low"], 1)

        def halve_b2(dve):
            rows = slice(0, PARTS * E)
            nc.vector.tensor_copy(b2_high[:, :], b2[:, :]).then_inc(sm["b2_high_set"], 1)
            dve.wait_ge(sm["b2_high_set"], 1)
            nc.vector.tensor_tensor(b2_low[:, :], b2[:, :], b2_high[:, :].bitcast(F32), ALU.subtract).then_inc(sm["b2_low_set"], 1)
            dve.wait_ge(sm["b2_low_set"], 1)
            nc.vector.tensor_scalar(b2_low[:, :], b2_low[:, :], K[rows, B2_LOW:B2_LOW + 1], None, ALU.mult).then_inc(sm["b2_scaled"], 1)
            dve.wait_ge(sm["b2_scaled"], 1)
            nc.vector.scalar_tensor_tensor(b2p[:, :], b2_high[:, :].bitcast(F32), K[rows, B2_HIGH:B2_HIGH + 1], b2_low[:, :],
                                           ALU.mult, ALU.add).then_inc(sm["b2_set"], 1)

        def ffn_low_rows(dve, n, u):
            dve.wait_ge(sm["f_xh"], n + 1)
            reached(dve, sm["f_hidden"], (n - 1) * E * C)
            nc.vector.tensor_tensor(xl[:, u, :], ps[:, PREP, :], xh[:, u, :].bitcast(F32), ALU.subtract).then_inc(sm["f_xl"], 1)

        def ffn_ranking(dve, n):
            dve.wait_ge(sm["f_logits_turned"], n + 1)
            nc.vector.tensor_tensor(lg[:, :, :], ps[:, routing_bank(n), P:2 * P].rearrange("p (j w) -> p j w", w=W)[:, :, 0:E],
                                    bg[:, :].unsqueeze(1).to_broadcast([P, J, E]), ALU.add).then_inc(sm["f_lg"], 1)
            dve.wait_ge(sm["f_lg"], n + 1)
            other = lg[:, :, :].unsqueeze(2).to_broadcast([P, J, E, E])
            own = lg[:, :, :].unsqueeze(3).to_broadcast([P, J, E, E])
            reached(dve, sm["f_ranks"], n)
            nc.vector.tensor_tensor(equal[:, :, :, :], other, own, ALU.is_equal).then_inc(sm["f_equal"], 1)
            nc.vector.tensor_tensor(before[:, :, :, :], other, own, ALU.is_gt).then_inc(sm["f_before"], 1)
            nc.vector.tensor_reduce(top[:, :], lg[:, :, :], AX.X, ALU.max).then_inc(sm["f_top"], 1)
            dve.wait_ge(sm["f_top"], n + 1)
            nc.vector.tensor_tensor(below[:, :, :], lg[:, :, :], top[:, :].unsqueeze(2).to_broadcast([P, J, E]),
                                    ALU.subtract).then_inc(sm["f_below"], 1)

        def ffn_gating(dve, n):
            dve.wait_ge(sm["f_ranks"], n + 1)
            nc.vector.tensor_reduce(rank[:, :, :], ranks[:, :, :, :], AX.X, ALU.add).then_inc(sm["f_rank"], 1)
            dve.wait_ge(sm["f_rank"], n + 1)
            dve.wait_ge(sm["f_weight"], n + 1)
            nc.vector.scalar_tensor_tensor(picked[:, :, :], rank[:, :, :], TOPK - 0.5, weight[:, :, :],
                                           ALU.is_lt, ALU.mult).then_inc(sm["f_picked"], 1)
            dve.wait_ge(sm["f_picked"], n + 1)
            nc.vector.tensor_reduce(total[:, :], picked[:, :, :], AX.X, ALU.add).then_inc(sm["f_total"], 1)
            dve.wait_ge(sm["f_total"], n + 1)
            nc.vector.reciprocal(inv[:, :], total[:, :]).then_inc(sm["f_inv"], 1)
            dve.wait_ge(sm["f_inv"], n + 1)
            reached(dve, sm["f_gturned"], n)
            nc.vector.scalar_tensor_tensor(gate_parts[:, :, 0, :], picked[:, :, :], 0.5,
                                           inv[:, :].unsqueeze(2).to_broadcast([P, J, E]), ALU.mult, ALU.mult).then_inc(sm["f_gate"], 1)

        def ffn_halve_gates(dve, n):
            dve.wait_ge(sm["f_gate"], n + 1)
            nc.vector.tensor_copy(gate_parts[:, :, 1:PARTS:2, :].bitcast(F32R),
                                  gate_parts[:, :, 0:1, :].to_broadcast([P, J, 2, E])).then_inc(sm["f_gate_high"], 1)
            dve.wait_ge(sm["f_gate_high"], n + 1)
            nc.vector.tensor_tensor(gate_parts[:, :, 2, :], gate_parts[:, :, 0, :], gate_parts[:, :, 1, :],
                                    ALU.subtract).then_inc(sm["f_parts"], 1)

        def ffn_norm_rows(dve, s, n, u):
            norm_rows(dve, "f_", s, n, u, lambda rows, u, j: (xnf[:, u, j, :], rows), [("f_turned", n - 1)])

        def ffn_vector(dve, p):
            def gate_hidden(n, u, e):
                m = n * E + e
                if e == 0:
                    dve.wait_ge(sm["f_gates_ahead"], 16 * (n + 1))
                if e == AHEAD:
                    dve.wait_ge(sm["f_gates_rest"], 16 * (n + 1))
                reached(dve, sm["f_low_pool"], m - 1)
                for c in range(C):
                    dve.wait_ge(sm["f_relu"], m * C + c + 1)
                    reached(dve, sm["f_high"], (m - 2) * C + c + 1)
                    nc.vector.tensor_tensor(gated[:, e % 2, c, :], hid[:, e % 2, c, :], gates_on_all[u][:, e, :],
                                            ALU.mult).then_inc(sm["f_gated"], 1)

            def low(n, e):
                m = n * E + e
                dve.wait_ge(sm["f_high"], m * C + C)
                reached(dve, sm["f_expert"], m - 1)
                nc.vector.tensor_tensor(gl[:, e % 2, 1, :], gated[:, e % 2, 1, :], gh[:, e % 2, 1, :].bitcast(F32),
                                        ALU.subtract).then_inc(sm["f_low_dve"], 1)

            def add(s, n, u):
                dve.wait_ge(sm["f_back"], n + 1)
                nc.vector.tensor_tensor(tokens(s), tokens(s), ps[:, OUTPUT[u], :], ALU.add).then_inc(sm["f_added"], 1)

            def body(i):
                for u in range(2):
                    s = i * 2 + u
                    n = s + p * S
                    first = isinstance(i, int) and s == 0
                    last = isinstance(i, int) and s == S - 1
                    later = not (isinstance(i, int) and s >= S - 2)
                    for e in range(E):
                        if e < E - 1:
                            gate_hidden(n, u, e + 1)
                        elif not last:
                            gate_hidden(n + 1, 1 - u, 0)
                        if e == 1 and not last:
                            ffn_gating(dve, n + 1)
                        if e == 2 and not last:
                            ffn_halve_gates(dve, n + 1)
                        if e == 4 and not first:
                            add(s - 1, n - 1, 1 - u)
                        if later:
                            if e == 0:
                                if p == 0 and first:
                                    dve.wait_ge(sm["x_rest"], 16)
                                norm_stats(dve, "f_", s + 2, n + 2, u)
                            if e == 3:
                                ffn_norm_rows(dve, s + 2, n + 2, u)
                            if e == 6:
                                ffn_low_rows(dve, n + 2, u)
                            if e == 7:
                                ffn_ranking(dve, n + 2)
                        if e < E - 1:
                            low(n, e + 1)
                        elif not last:
                            low(n + 1, 0)
                        if p == 0 and last:
                            if e == 1:
                                dve.wait_ge(sm["f_added"], 1)
                                norm_stats(dve, "a_", 0, 0, 0)
                            if e == 3:
                                attn_norm_rows(dve, 0, 0)
                            if e == 5:
                                attn_centre(dve, 0)
                            if e == 6:
                                attn_operands(dve, 0, 0)

            if p == 0:
                norm_stats(dve, "f_", 0, 0, 0)
                ffn_norm_rows(dve, 0, 0, 0)
                first_half_of_w1(dve)
                second_half_of_w1(dve)
                ffn_low_rows(dve, 0, 0)
                dve.wait_ge(sm["small_in"], 16 * 7)
                ffn_ranking(dve, 0)
                ffn_gating(dve, 0)
                ffn_halve_gates(dve, 0)
                halve_b2(dve)
                norm_stats(dve, "f_", 1, 1, 1)
                ffn_norm_rows(dve, 1, 1, 1)
            else:
                dve.wait_ge(sm["a_added"], S * G)
            ffn_low_rows(dve, p * S + 1, 1)
            ffn_ranking(dve, p * S + 1)
            gate_hidden(p * S, 0, 0)
            low(p * S, 0)
            pairs_of_sequences(dve, body)
            add(S - 1, p * S + S - 1, 1)

        def ffn_copy_rows(act, n, u):
            act.wait_ge(sm["f_turned"], n + 1)
            reached(act, sm["f_logits"], n)
            nc.scalar.activation(xnT[:, :], ps[:, PREP, :], ACT.Copy).then_inc(sm["f_xnT"], 1)

        def ffn_copy_high(act, n, u):
            reached(act, sm["f_hidden"], (n - 1) * E * C)
            nc.scalar.activation(xh[:, u, :], ps[:, PREP, :], ACT.Copy).then_inc(sm["f_xh"], 1)

        def ffn_copy_logits(act, n):
            act.wait_ge(sm["f_logits"], n + 1)
            reached(act, sm["f_logits_turned"], n)
            nc.scalar.activation(logit_rows[:, :], ps[:, routing_bank(n), 0:P], ACT.Copy).then_inc(sm["f_logit_rows"], 1)

        def ffn_weights(act, n):
            act.wait_ge(sm["f_below"], n + 1)
            reached(act, sm["f_picked"], n)
            nc.scalar.activation(weight[:, :, :], below[:, :, :], ACT.Exp).then_inc(sm["f_weight"], 1)

        def ffn_copy_gates(act, n, u):
            act.wait_ge(sm["f_gturned"], n + 1)
            reached(act, sm["f_expert"], (n - 1) * E)
            nc.scalar.activation(gateT[:, u, :], ps[0:PARTS * E, routing_bank(n), :], ACT.Copy).then_inc(sm["f_gateT"], 1)
            reached(act, sm["f_gates_stored"], 16 * (n - 1))
            nc.scalar.activation(gate_rows[:, u, :], ps[0:E, routing_bank(n), :], ACT.Copy).then_inc(sm["f_gate_rows"], 1)

        def ffn_scalar(act, p):
            def relu(n, e):
                m = n * E + e
                for c in range(C):
                    reached(act, sm["f_gated"], (m - 2) * C + c + 1)
                    act.wait_ge(sm["f_hidden"], m * C + c + 1)
                    nc.scalar.activation(hid[:, e % 2, c, :], ps[:, C * (e % 2) + c, :], ACT.Relu,
                                         bias=b1[:, e * C + c:e * C + c + 1]).then_inc(sm["f_relu"], 1)

            def high(n, e):
                m = n * E + e
                reached(act, sm["f_expert"], m - 1)
                for c in range(C):
                    act.wait_ge(sm["f_gated"], m * C + c + 1)
                    nc.scalar.activation(gh[:, e % 2, c, :], gated[:, e % 2, c, :], ACT.Copy).then_inc(sm["f_high"], 1)

            def output(n, u):
                act.wait_ge(sm["f_expert"], n * E + E)
                reached(act, sm["f_back"], n)
                nc.scalar.activation(yT[:, :], ps[:, OUTPUT[u], :], ACT.Copy).then_inc(sm["f_output"], 1)

            def body(i):
                for u in range(2):
                    n = i * 2 + u + p * S
                    first = isinstance(i, int) and i * 2 + u == 0
                    last = isinstance(i, int) and i * 2 + u == S - 1
                    later = not (isinstance(i, int) and i * 2 + u >= S - 2)
                    for e in range(E):
                        if e == 0 and not first:
                            output(n - 1, 1 - u)
                        if e < E - 2:
                            relu(n, e + 2)
                        elif not last:
                            relu(n + 1, e + 2 - E)
                        if e < E - 1:
                            high(n, e + 1)
                        elif not last:
                            high(n + 1, 0)
                        if e == AHEAD + 1 and not last:
                            ffn_copy_gates(act, n + 1, 1 - u)
                        if e == 4 and later:
                            ffn_copy_rows(act, n + 2, u)
                        if e == 5 and later:
                            ffn_copy_high(act, n + 2, u)
                            ffn_copy_logits(act, n + 2)
                        if e == 0 and not last:
                            ffn_weights(act, n + 1)

            if p == 0:
                ffn_copy_rows(act, 0, 0)
                ffn_copy_high(act, 0, 0)
                act.wait_ge(sm["b1_turned"], 1)
                nc.scalar.activation(b1[:, :], ps[:, TURN, 0:E * C], ACT.Copy).then_inc(sm["b1_set"], 1)
                ffn_copy_logits(act, 0)
                first_half_of_w2(act)
                ffn_weights(act, 0)
            ffn_copy_gates(act, p * S, 0)
            if p == 0:
                act.wait_ge(sm["b1_set"], 1)
            relu(p * S, 0)
            relu(p * S, 1)
            ffn_copy_rows(act, p * S + 1, 1)
            ffn_copy_high(act, p * S + 1, 1)
            ffn_copy_logits(act, p * S + 1)
            high(p * S, 0)
            pairs_of_sequences(act, body)
            output(p * S + S - 1, 1)

        def ffn_ties(pool, n):
            pool.wait_ge(sm["f_equal"], n + 1)
            tri = K[:, TRI:TRI + E * E].unsqueeze(1).to_broadcast([P, J, E * E])
            nc.gpsimd.tensor_tensor(tied[:, :, :, :].rearrange("p j e f -> p j (e f)"),
                                    equal[:, :, :, :].rearrange("p j e f -> p j (e f)"), tri, ALU.mult).then_inc(sm["f_tied"], 1)
            pool.wait_ge(sm["f_before"], n + 1)
            pool.wait_ge(sm["f_tied"], n + 1)
            reached(pool, sm["f_rank"], n)
            nc.gpsimd.tensor_tensor(ranks[:, :, :, :], before[:, :, :, :], tied[:, :, :, :], ALU.add).then_inc(sm["f_ranks"], 1)

        def ffn_gpsimd(pool, p):
            def low(n, e):
                m = n * E + e
                pool.wait_ge(sm["f_high"], m * C + 1)
                reached(pool, sm["f_expert"], m - 1)
                nc.gpsimd.tensor_tensor(gl[:, e % 2, 0, :], gated[:, e % 2, 0, :], gh[:, e % 2, 0, :].bitcast(F32),
                                        ALU.subtract).then_inc(sm["f_low_pool"], 1)

            def body(i):
                for u in range(2):
                    n = i * 2 + u + p * S
                    last = isinstance(i, int) and i * 2 + u == S - 1
                    later = not (isinstance(i, int) and i * 2 + u >= S - 2)
                    for e in range(E):
                        if e < E - 1:
                            low(n, e + 1)
                        elif not last:
                            low(n + 1, 0)
                        if later and e == 0:
                            norm_means(pool, "f_", n + 2, u)
                        if later and e == 1:
                            norm_variances(pool, "f_", n + 2)
                        if later and e == 2:
                            norm_powers(pool, "f_", n + 2, u)
                        if later and e == 7:
                            ffn_ties(pool, n + 2)
                        if p == 0 and last and e == 1:
                            norm_pool(pool, "a_", 0, 0)
                        if p == 0 and last and e == 5:
                            attn_square_rows(pool, 0)

            if p == 0:
                norm_pool(pool, "f_", 0, 0)
                ffn_ties(pool, 0)
                second_half_of_w2(pool)
                norm_pool(pool, "f_", 1, 1)
            ffn_ties(pool, p * S + 1)
            low(p * S, 0)
            pairs_of_sequences(pool, body)


        def attn_turn(pe, g, s, u, hg):
            if hg == 0:
                pe.wait_ge(sm["a_xn"], s + 1)
            reached(pe, sm["a_query"], g)
            for j in range(J):
                rows = xna[:, u, j, hg * Q:(hg + 1) * Q, :, :].rearrange("p q r i -> p (q r i)")
                ins = nc.tensor.transpose(ps[:, PREP, j * P:(j + 1) * P], rows, ident)
            ins.then_inc(sm["a_turned"], 1)

        def attn_norms(pe, g):
            pe.wait_ge(sm["a_square"], g + 1)
            nc.tensor.matmul(ps[:, PREP, :], block_bf[:, :], square[:, :], start=True, stop=True).then_inc(sm["a_norms"], 1)

        def attn_tensor(pe):
            def scores(g, b, kk):
                j, half = kk // 2, kk % 2
                if kk == 0:
                    pe.wait_ge(sm["a_query"], g + 1)
                reached(pe, sm["a_probs"], g * STAGES + kk - 1)
                at = slice(half * 2 * W, (half + 1) * 2 * W)
                for odd, keyed in enumerate((key_even, key_odd)):
                    ins = nc.tensor.matmul(ps[:, 2 * (kk % 2) + odd, :], keyed[at, b, j * P:(j + 1) * P], query[at, b, :],
                                           start=True, stop=True)
                ins.then_inc(sm["a_scores"], 1)

            def mix(g, s, u, b, hg, kk):
                j, half = kk // 2, kk % 2
                if kk == 0:
                    pe.wait_ge(sm["a_value"], s + 1)
                    reached(pe, sm["a_copied"], g - 1)
                pe.wait_ge(sm["a_probs"], g * STAGES + kk + 1)
                for odd in range(2):
                    q = 2 * half + odd
                    ins = nc.tensor.matmul(ps[q * W:(q + 1) * W, 4 + b, :], value[:, u, j, hg * Q + q, :],
                                           ring[kk][:, odd, :], start=(j == 0), stop=(j == J - 1))
                ins.then_inc(sm["a_mixed"], 1)

            def back(g, b):
                pe.wait_ge(sm["a_copied"], g + 1)
                reached(pe, sm["a_normed"], g)
                for j in range(J):
                    ins = nc.tensor.transpose(ps[:, TURN, j * P:(j + 1) * P], mixed[:, b, j * P:(j + 1) * P], ident)
                ins.then_inc(sm["a_back"], 1)

            def body(i):
                for t in range(2 * G):
                    g, u, hg, b = i * 2 * G + t, t // G, t % G, t % 2
                    first = isinstance(i, int) and i * 2 * G + t == 0
                    last = isinstance(i, int) and i * 2 * G + t == S * G - 1
                    for kk in range(STAGES):
                        if kk < STAGES - 2:
                            scores(g, b, kk + 2)
                        elif not last:
                            scores(g + 1, 1 - b, kk + 2 - STAGES)
                        if kk % 2 == 1:
                            mix(g, i * 2 + u, u, b, hg, kk - 1)
                            mix(g, i * 2 + u, u, b, hg, kk)
                        if kk == 2 and not last:
                            attn_norms(pe, g + 1)
                        if kk == 4 and not first:
                            back(g - 1, 1 - b)
                        if kk == 6 and not last and not (isinstance(i, int) and i * 2 * G + t == S * G - 2):
                            attn_turn(pe, g + 2, i * 2 + (t + 2) // G, (t + 2) // G % 2, (t + 2) % G)
                        if groups_after(g) == 1 and kk == 7:
                            ffn_turn(pe, S, 0)
                        if groups_after(g) == 0 and kk == 1:
                            ffn_logits(pe, S)
                        if groups_after(g) == 0 and kk == 3:
                            ffn_turn_logits(pe, S)

            pe.wait_ge(sm["f_relu"], S * E * C)
            scores(0, 0, 0)
            scores(0, 0, 1)
            ffn_back(pe, S - 1, 1)
            pe.wait_ge(sm["f_added"], S)
            pairs_of_sequences(pe, body)
            ffn_turn_gates(pe, S)
            back(S * G - 1, 1)

        def attn_centre(dve, g):
            dve.wait_ge(sm["a_turned"], g + 1)
            nc.vector.reduce_sum(negsum[:, :], ps[:, PREP, :], AX.X, negate=True).then_inc(sm["a_sum"], 1)
            dve.wait_ge(sm["a_sum"], g + 1)
            reached(dve, sm["a_square"], g)
            nc.vector.tensor_scalar(cent[:, :], ps[:, PREP, :], CENTRED, negsum[:, :], ALU.mult, ALU.add).then_inc(sm["a_cent"], 1)

        def attn_operands(dve, g, b):
            dve.wait_ge(sm["a_cent"], g + 1)
            nc.vector.tensor_copy(high[:, :], cent[:, :]).then_inc(sm["a_high"], 1)
            dve.wait_ge(sm["a_high"], g + 1)
            nc.vector.scalar_tensor_tensor(keys[:, :], high[:, :], const(KEY_LO), cent[:, :],
                                           ALU.mult, ALU.add).then_inc(sm["a_keys"], 1)
            nc.vector.scalar_tensor_tensor(part[:, :], high[:, :], const(QUERY_LO), cent[:, :],
                                           ALU.mult, ALU.add).then_inc(sm["a_part"], 1)
            dve.wait_ge(sm["a_keys"], g + 1)
            reached(dve, sm["a_scores"], (g - 1) * STAGES)
            nc.vector.tensor_scalar(key_even[:, b, :], keys[:, :], const(KEEP_EVEN), const(UNIT_EVEN), ALU.mult, ALU.add)
            nc.vector.tensor_scalar(key_odd[:, b, :], keys[:, :], const(KEEP_ODD), const(UNIT_ODD), ALU.mult, ALU.add).then_inc(sm["a_keyed"], 1)
            dve.wait_ge(sm["a_part"], g + 1)
            dve.wait_ge(sm["a_norms"], g + 1)
            nc.vector.scalar_tensor_tensor(query[:, b, :], ps[:, PREP, :], const(SHIFT_ROW), part[:, :],
                                           ALU.mult, ALU.add).then_inc(sm["a_query"], 1)

        def attn_norm_rows(dve, s, u):
            def copies(rows, u, j):
                rows = rows.rearrange("p (h i) -> p h i", i=HD).unsqueeze(2).to_broadcast([P, H, REP, HD])
                return xna[:, u, j, :, :, :], rows
            norm_rows(dve, "a_", s, s, u, copies, [("a_turned", (s - 1) * G), ("a_value", s - 1)])

        def attn_vector(dve):
            def copy(g, b):
                dve.wait_ge(sm["a_mixed"], g * STAGES + STAGES)
                reached(dve, sm["a_back"], g - 1)
                nc.vector.tensor_copy(mixed[:, b, :], ps[:, 4 + b, :]).then_inc(sm["a_copied"], 1)

            def finish(g, s, hg):
                dve.wait_ge(sm["a_back"], g + 1)
                back = ps[:, TURN, :].rearrange("p (j q w) -> p j q w", j=J, q=Q)
                nc.vector.reciprocal(recip[:, :, :], back[:, :, :, HD]).then_inc(sm["a_recip"], 1)
                dve.wait_ge(sm["a_recip"], g + 1)
                nc.vector.tensor_tensor(normed[:, :, :, :], back[:, :, :, 0:HD],
                                        recip[:, :, :].unsqueeze(3).to_broadcast([P, J, Q, HD]), ALU.mult).then_inc(sm["a_normed"], 1)
                dve.wait_ge(sm["a_normed"], g + 1)
                rows = tokens(s).rearrange("p (j d) -> p j d", j=J)[:, :, hg * Q * HD:(hg + 1) * Q * HD]
                nc.vector.tensor_tensor(rows, rows, normed[:, :, :, :].rearrange("p j q i -> p j (q i)"),
                                        ALU.add).then_inc(sm["a_added"], 1)

            def body(i):
                for t in range(2 * G):
                    g, s, u, hg, b = i * 2 * G + t, i * 2 + t // G, t // G, t % G, t % 2
                    first = isinstance(i, int) and i * 2 * G + t == 0
                    last = isinstance(i, int) and i * 2 * G + t == S * G - 1
                    if not last:
                        attn_centre(dve, g + 1)
                    if not first:
                        copy(g - 1, 1 - b)
                    if not last:
                        attn_operands(dve, g + 1, 1 - b)
                    if groups_after(g) == 0:
                        ffn_low_rows(dve, S, 0)
                        ffn_ranking(dve, S)
                    if not first:
                        finish(g - 1, i * 2 + (t - 1) // G, (t - 1) % G)
                    if not (isinstance(i, int) and s == S - 1):
                        if hg == 0:
                            norm_stats(dve, "a_", s + 1, s + 1, 1 - u)
                        if hg == 1:
                            attn_norm_rows(dve, s + 1, 1 - u)
                    if groups_after(g) == 2:
                        dve.wait_ge(sm["a_added"], 2 * G)
                        norm_stats(dve, "f_", 0, S, 0)
                    if groups_after(g) == 1:
                        ffn_norm_rows(dve, 0, S, 0)
                        norm_stats(dve, "f_", 1, S + 1, 1)
                    if groups_after(g) == 0:
                        ffn_gating(dve, S)
                        ffn_halve_gates(dve, S)
                        ffn_norm_rows(dve, 1, S + 1, 1)

            dve.wait_ge(sm["f_added"], S)
            pairs_of_sequences(dve, body)
            copy(S * G - 1, 1)
            finish(S * G - 1, S - 1, G - 1)

        def attn_scalar(act):
            def body(i):
                for t in range(2 * G):
                    g = i * 2 * G + t
                    for kk in range(STAGES):
                        act.wait_ge(sm["a_scores"], g * STAGES + kk + 1)
                        reached(act, sm["a_mixed"], (g - 1) * STAGES + kk + 1)
                        nc.scalar.activation(ring[kk], ps[:, 2 * (kk % 2):2 * (kk % 2) + 2, :], ACT.Exp,
                                             bias=const(MINUS_SHIFT), scale=SCORE).then_inc(sm["a_probs"], 1)
                        if groups_after(g) == 0 and kk == 0:
                            ffn_copy_rows(act, S, 0)
                            ffn_copy_high(act, S, 0)
                        if groups_after(g) == 0 and kk == 2:
                            ffn_copy_logits(act, S)
                        if groups_after(g) == 0 and kk == 6:
                            ffn_weights(act, S)
            pairs_of_sequences(act, body)

        def attn_square_rows(pool, g):
            pool.wait_ge(sm["a_cent"], g + 1)
            reached(pool, sm["a_norms"], g)
            nc.gpsimd.tensor_tensor(square[:, :], cent[:, :], cent[:, :], ALU.mult).then_inc(sm["a_square"], 1)

        def attn_gpsimd(pool):
            def values_due(s):
                pool.wait_ge(sm["a_xn"], s + 1)
                reached(pool, sm["a_mixed"], (s - 1) * G * STAGES)

            def values(u):
                for j in range(J):
                    ins = nc.gpsimd.tensor_copy(value[:, u, j, :, 0:HD], xna[:, u, j, :, 0, :])
                ins.then_inc(sm["a_value"], 1)

            def body(i):
                for t in range(2 * G):
                    g, s, u, hg = i * 2 * G + t, i * 2 + t // G, t // G, t % G
                    more = not (isinstance(i, int) and s == S - 1)
                    if hg == 2 and more:
                        values_due(s + 1)
                    if not (isinstance(i, int) and i * 2 * G + t == S * G - 1):
                        attn_square_rows(pool, g + 1)
                    if hg == 0 and more:
                        norm_pool(pool, "a_", s + 1, 1 - u)
                    if hg == 2 and more:
                        values(1 - u)
                    if groups_after(g) == 2:
                        norm_pool(pool, "f_", S, 0)
                    if groups_after(g) == 1:
                        norm_pool(pool, "f_", S + 1, 1)
                    if groups_after(g) == 0:
                        ffn_ties(pool, S)

            values_due(0)
            values(0)
            pairs_of_sequences(pool, body)

        @block.gpsimd
        def _(pool):
            nc.gpsimd.memset(WG[:, :], 0.0).then_inc(sm["wg_cleared"], 1)
            nc.gpsimd.memset(value[:, :, :, :, :], 0.0).then_inc(sm["value_set"], 1)
            pool.wait_ge(sm["value_set"], 1)
            nc.gpsimd.memset(value[:, :, :, :, HD:HD + 1], 1.0).then_inc(sm["value_set"], 1)
            pool.wait_ge(sm["value_set"], 2)
            pool.wait_ge(sm["const_in"], 16)
            ffn_gpsimd(pool, 0)
            attn_gpsimd(pool)
            ffn_gpsimd(pool, 1)

        @block.tensor
        def _(pe):
            pe.wait_ge(sm["const_in"], 16)
            pe.wait_ge(sm["block_set"], 1)
            ffn_tensor(pe, 0)
            attn_tensor(pe)
            pe.wait_ge(sm["a_probs"], S * G * STAGES)
            pe.wait_ge(sm["a_copied"], S * G)
            ffn_tensor(pe, 1)
            ffn_back(pe, 2 * S - 1, 1)

        @block.scalar
        def _(act):
            act.dma_start(K[:, :], const_in).then_inc(sm["const_in"], 16)
            act.dma_start(W1[:, :, :], w1_in.rearrange("e d f -> d e f")).then_inc(sm["w1_in"], 16)
            act.dma_start(W2[:, :, :, :], w2_in.rearrange("e (c p) d -> p e c d", c=C)).then_inc(sm["w2_in"], 16)
            ffn_scalar(act, 0)
            attn_scalar(act)
            ffn_scalar(act, 1)

        @block.vector
        def _(dve):
            dve.wait_ge(sm["const_in"], 16)
            nc.vector.tensor_copy(block_bf[:, :], K[:, BLOCK:BLOCK + P]).then_inc(sm["block_set"], 1)
            dve.wait_ge(sm["x_first"], 16)
            ffn_vector(dve, 0)
            attn_vector(dve)
            ffn_vector(dve, 1)


def kernel(**inputs):
    import concourse.bacc as bacc
    from concourse.bass_utils import run_bass_kernel_spmd as run

    nc = bacc.Bacc("TRN2", target_bir_lowering=False, num_devices=1)
    names = ["L0_attn_x", "L0_ffn_Wg", "L0_ffn_bg", "L0_ffn_W1", "L0_ffn_b1", "L0_ffn_W2", "L0_ffn_b2"]
    arrays = {"in_" + n: np.ascontiguousarray(inputs[n]) for n in names}
    arrays["in_constants"] = constants()
    args = [nc.dram_tensor(n, a.shape, F32, kind="ExternalInput").ap() for n, a in arrays.items()]
    out = nc.dram_tensor("out", (S, T, D), F32, kind="ExternalOutput").ap()
    gates_dram = nc.dram_tensor("gates", (2, E, T), F32, kind="Internal").ap()
    build(nc, *args, gates_dram, out)
    return run(nc, [arrays], core_ids=[0]).results[0]["out"]
```
